# Optimizing a Trainium2 kernel written in Bass

```python
import numpy as np
import jax
import jax.numpy as jnp

def _softmax(x, axis=-1):
    return jax.nn.softmax(x, axis=axis)

def _gelu(x):
    return jax.nn.gelu(x, approximate=True)

def _silu(x):
    return jax.nn.silu(x)

def _sigmoid(x):
    return jax.nn.sigmoid(x)

def _layernorm(x, axis=-1, eps=1e-05):
    m = jnp.mean(x, axis=axis, keepdims=True)
    v = jnp.var(x, axis=axis, keepdims=True)
    return (x - m) / jnp.sqrt(v + eps)

def _scatter_add(tgt, idx, src, axis=0):
    return tgt.at[idx].add(src)

def _segment_sum(src, seg, n):
    return jax.ops.segment_sum(src, seg, n)
kernel_name = 'mk_early_fusion_embed_d1_tok_img512_r4_80a040'

def setup_inputs(seed: int=0):
    np.random.seed(seed)
    _w = jnp.asarray

    def _rec_inputs():
        import jax
        import jax.numpy as jnp
        _rk = jax.random.key(seed)
        x = -0.00136767 + 1.0008 * jax.random.normal(jax.random.fold_in(_rk, 1), (4, 128, 50, 3), jnp.float32)
        x_txt = jax.random.randint(jax.random.fold_in(_rk, 51), (4, 512), 0, 8000, jnp.int32)
        return (x, x_txt)
    x, x_txt = _rec_inputs()

    def _L0_tok_setup():
        import jax, jax.numpy as jnp
        import numpy as np
        J = 50
        HEADS = 4
        DIMS = [3, 64, 128, 64]
        POSE_DIM = 128
        B, T = (16, 128)

        def build_edge_index():
            e = []
            for i in range(J - 1):
                e.append((i, i + 1))
                e.append((i + 1, i))
            for i in range(J):
                e.append((i, i))
            e = sorted(e)
            return jnp.array(e, dtype=jnp.int32).T

        def _layer_norm(x, g, b, eps=1e-05):
            mu = jnp.mean(x, axis=-1, keepdims=True)
            var = jnp.mean(jnp.square(x - mu), axis=-1, keepdims=True)
            return (x - mu) * jax.lax.rsqrt(var + eps) * g + b

        def _gat(x, src, dst, W, a_s, a_d, bias):
            G, Jn, _ = x.shape
            H, C = a_s.shape
            h = (x @ W).reshape(G, Jn, H, C)
            es = jnp.einsum('gjhc,hc->gjh', h, a_s)[:, src]
            ed = jnp.einsum('gjhc,hc->gjh', h, a_d)[:, dst]
            e = jax.nn.leaky_relu(es + ed, 0.2)
            m = jnp.full((G, Jn, H), -jnp.inf, e.dtype).at[:, dst].max(e)
            m = jax.lax.stop_gradient(m)
            w = jnp.exp(e - m[:, dst])
            den = jnp.zeros((G, Jn, H), e.dtype).at[:, dst].add(w)
            alpha = w / den[:, dst]
            out = jnp.zeros((G, Jn, H, C), e.dtype).at[:, dst].add(alpha[..., None] * h[:, src])
            return out.reshape(G, Jn, H * C) + bias

        def _forward(pose_seq, layers, fpW, fpb, fng, fnb, edge_index):
            Bb, Tt = (pose_seq.shape[0], pose_seq.shape[1])
            x = pose_seq.reshape(Bb * Tt, J, 3)
            src, dst = (edge_index[0], edge_index[1])
            for W, a_s, a_d, bg, R, g, b in layers:
                h = _gat(x, src, dst, W, a_s, a_d, bg)
                res = x @ R
                x = jax.nn.gelu(_layer_norm(h + res, g, b), approximate=False)
            x = x.reshape(Bb * Tt, J * DIMS[-1]) @ fpW + fpb
            x = _layer_norm(x, fng, fnb)
            return x.reshape(Bb, Tt, POSE_DIM)
        key = jax.random.key(seed)
        ks = iter(jax.random.split(key, 64))

        def nrm(shape, s):
            return jax.random.normal(next(ks), shape, jnp.float32) * s
        inp = {'pose_seq': jax.random.normal(next(ks), (B, T, J, 3), jnp.float32)}
        for i in range(3):
            din, dout = (DIMS[i], DIMS[i + 1])
            C = dout // HEADS
            inp[f'W{i}'] = nrm((din, dout), din ** (-0.5))
            inp[f'as{i}'] = nrm((HEADS, C), 0.1)
            inp[f'ad{i}'] = nrm((HEADS, C), 0.1)
            inp[f'bg{i}'] = jnp.zeros((dout,), jnp.float32)
            inp[f'R{i}'] = nrm((din, dout), din ** (-0.5))
            inp[f'g{i}'] = jnp.ones((dout,), jnp.float32)
            inp[f'b{i}'] = jnp.zeros((dout,), jnp.float32)
        inp['fpW'] = nrm((J * DIMS[-1], POSE_DIM), (J * DIMS[-1]) ** (-0.5))
        inp['fpb'] = jnp.zeros((POSE_DIM,), jnp.float32)
        inp['fng'] = jnp.ones((POSE_DIM,), jnp.float32)
        inp['fnb'] = jnp.zeros((POSE_DIM,), jnp.float32)
        inp['edge_index'] = build_edge_index()
        return inp
    _L0_tok_all = _L0_tok_setup()
    _L0_tok_in = {k: v for k, v in _L0_tok_all.items() if k in ('W0', 'as0', 'ad0', 'bg0', 'R0', 'g0', 'b0', 'W1', 'as1', 'ad1', 'bg1', 'R1', 'g1', 'b1', 'W2', 'as2', 'ad2', 'bg2', 'R2', 'g2', 'b2', 'fpW', 'fpb', 'fng', 'fnb', 'edge_index')}
    del _L0_tok_all

    def _L0_txt_setup():
        import jax, jax.numpy as jnp
        import numpy as np
        VOCAB = 8000
        EMB = 128
        K = 3
        B, T = (8, 1024)
        key = jax.random.key(seed)
        k_ids, k_w = jax.random.split(key)
        token_ids = jax.random.randint(k_ids, (B, T), 0, VOCAB, dtype=jnp.int64)
        conv_w = jax.random.normal(k_w, (EMB, VOCAB, K), dtype=jnp.float32) * 0.02
        return {'token_ids': token_ids, 'conv_w': conv_w}
    _L0_txt_all = _L0_txt_setup()
    _L0_txt_in = {k: v for k, v in _L0_txt_all.items() if k in ('conv_w',)}
    del _L0_txt_all

    def _L0_attn_setup():
        import jax, jax.numpy as jnp
        import numpy as np
        L = 4
        D_MODEL = 128
        D_INNER = 256
        D_STATE = 64
        D_CONV = 4
        BATCH = 64
        SEQ = 117

        def _layer_norm(v, g, b, eps=1e-05):
            mu = v.mean(-1, keepdims=True)
            var = ((v - mu) ** 2).mean(-1, keepdims=True)
            return (v - mu) / jnp.sqrt(var + eps) * g + b

        def _mamba_block(x, in_w, cw, cb, xw, dw, db, alog, dvec, ow, g, b):
            xz = x @ in_w
            xm, z = jnp.split(xz, 2, axis=-1)
            lhs = xm.transpose(0, 2, 1)
            conv = jax.lax.conv_general_dilated(lhs, cw, window_strides=(1,), padding=[(D_CONV - 1, 0)], dimension_numbers=('NCH', 'OIH', 'NCH'), feature_group_count=D_INNER)
            xc = jax.nn.silu(conv.transpose(0, 2, 1) + cb)
            Bp, Cp = jnp.split(xc @ xw, 2, axis=-1)
            dt = jax.nn.softplus(xc @ dw + db)
            A = -jnp.exp(alog)

            def step(h, inp):
                xt, dtt, Bt, Ct = inp
                h = jnp.exp(dtt[..., None] * A) * h + (dtt * xt)[..., None] * Bt[:, None, :]
                y = jnp.einsum('bdn,bn->bd', h, Ct) + dvec * xt
                return (h, y)
            h0 = jnp.zeros((x.shape[0], D_INNER, D_STATE), x.dtype)
            xs = (xc.transpose(1, 0, 2), dt.transpose(1, 0, 2), Bp.transpose(1, 0, 2), Cp.transpose(1, 0, 2))
            _, ys = jax.lax.scan(step, h0, xs)
            y = ys.transpose(1, 0, 2) * jax.nn.silu(z)
            out = y @ ow
            return _layer_norm(out + x, g, b)
        key = jax.random.key(seed)
        ks = jax.random.split(key, 7)
        s = 0.02
        x = jax.random.normal(ks[0], (BATCH, SEQ, D_MODEL), jnp.float32)
        in_proj_w = jax.random.normal(ks[1], (L, D_MODEL, 2 * D_INNER), jnp.float32) * s
        conv_w = jax.random.normal(ks[2], (L, D_INNER, 1, D_CONV), jnp.float32) * s
        conv_b = jnp.zeros((L, D_INNER), jnp.float32)
        x_proj_w = jax.random.normal(ks[3], (L, D_INNER, 2 * D_STATE), jnp.float32) * s
        dt_w = jax.random.normal(ks[4], (L, D_INNER, D_INNER), jnp.float32) * s
        dt_b = jnp.full((L, D_INNER), -1.0, jnp.float32)
        A_log = jnp.tile(jnp.log(jnp.arange(1.0, D_STATE + 1, dtype=jnp.float32)), (L, D_INNER, 1))
        D_param = jnp.ones((L, D_INNER), jnp.float32)
        out_w = jax.random.normal(ks[5], (L, D_INNER, D_MODEL), jnp.float32) * s
        ln_g = jnp.ones((L, D_MODEL), jnp.float32)
        ln_b = jnp.zeros((L, D_MODEL), jnp.float32)
        return {'x': x, 'in_proj_w': in_proj_w, 'conv_w': conv_w, 'conv_b': conv_b, 'x_proj_w': x_proj_w, 'dt_w': dt_w, 'dt_b': dt_b, 'A_log': A_log, 'D_param': D_param, 'out_w': out_w, 'ln_g': ln_g, 'ln_b': ln_b}
    _L0_attn_all = _L0_attn_setup()
    _L0_attn_in = {k: v for k, v in _L0_attn_all.items() if k in ('in_proj_w', 'conv_w', 'conv_b', 'x_proj_w', 'dt_w', 'dt_b', 'A_log', 'D_param', 'out_w', 'ln_g', 'ln_b')}
    del _L0_attn_all

    def _L0_ffn_setup():
        import jax, jax.numpy as jnp
        import numpy as np
        from jax import lax
        N, M, DIM, HEADS, TOPK = (4, 512, 128, 8, 16)

        def _split_heads(t, h):
            n, m, c = t.shape
            return t.reshape(n, m, h, c // h).transpose(0, 2, 1, 3).reshape(n * h, m, c // h)
        key = jax.random.key(seed)
        ks = jax.random.split(key, 7)
        f = lambda k, s, sc=1.0: jax.random.normal(k, s, dtype=jnp.float32) * sc
        return {'x': f(ks[0], (N, M, DIM)), 'pos_w': f(ks[1], (DIM, 1, 3), 0.1), 'pos_b': f(ks[2], (DIM,), 0.02), 'qkv_w': f(ks[3], (3 * DIM, DIM), 0.02), 'qkv_b': f(ks[4], (3 * DIM,), 0.02), 'wo_w': f(ks[5], (DIM, DIM), 0.02), 'wo_b': f(ks[6], (DIM,), 0.02)}
    _L0_ffn_all = _L0_ffn_setup()
    _L0_ffn_in = {k: v for k, v in _L0_ffn_all.items() if k in ('pos_w', 'pos_b', 'qkv_w', 'qkv_b', 'wo_w', 'wo_b')}
    del _L0_ffn_all
    return {'x': x, 'x_txt': x_txt, 'L0_tok_W0': _L0_tok_in['W0'], 'L0_tok_as0': _L0_tok_in['as0'], 'L0_tok_ad0': _L0_tok_in['ad0'], 'L0_tok_bg0': _L0_tok_in['bg0'], 'L0_tok_R0': _L0_tok_in['R0'], 'L0_tok_g0': _L0_tok_in['g0'], 'L0_tok_b0': _L0_tok_in['b0'], 'L0_tok_W1': _L0_tok_in['W1'], 'L0_tok_as1': _L0_tok_in['as1'], 'L0_tok_ad1': _L0_tok_in['ad1'], 'L0_tok_bg1': _L0_tok_in['bg1'], 'L0_tok_R1': _L0_tok_in['R1'], 'L0_tok_g1': _L0_tok_in['g1'], 'L0_tok_b1': _L0_tok_in['b1'], 'L0_tok_W2': _L0_tok_in['W2'], 'L0_tok_as2': _L0_tok_in['as2'], 'L0_tok_ad2': _L0_tok_in['ad2'], 'L0_tok_bg2': _L0_tok_in['bg2'], 'L0_tok_R2': _L0_tok_in['R2'], 'L0_tok_g2': _L0_tok_in['g2'], 'L0_tok_b2': _L0_tok_in['b2'], 'L0_tok_fpW': _L0_tok_in['fpW'], 'L0_tok_fpb': _L0_tok_in['fpb'], 'L0_tok_fng': _L0_tok_in['fng'], 'L0_tok_fnb': _L0_tok_in['fnb'], 'L0_tok_edge_index': _L0_tok_in['edge_index'], 'L0_txt_conv_w': _L0_txt_in['conv_w'], 'L0_attn_in_proj_w': _L0_attn_in['in_proj_w'], 'L0_attn_conv_w': _L0_attn_in['conv_w'], 'L0_attn_conv_b': _L0_attn_in['conv_b'], 'L0_attn_x_proj_w': _L0_attn_in['x_proj_w'], 'L0_attn_dt_w': _L0_attn_in['dt_w'], 'L0_attn_dt_b': _L0_attn_in['dt_b'], 'L0_attn_A_log': _L0_attn_in['A_log'], 'L0_attn_D_param': _L0_attn_in['D_param'], 'L0_attn_out_w': _L0_attn_in['out_w'], 'L0_attn_ln_g': _L0_attn_in['ln_g'], 'L0_attn_ln_b': _L0_attn_in['ln_b'], 'L0_ffn_pos_w': _L0_ffn_in['pos_w'], 'L0_ffn_pos_b': _L0_ffn_in['pos_b'], 'L0_ffn_qkv_w': _L0_ffn_in['qkv_w'], 'L0_ffn_qkv_b': _L0_ffn_in['qkv_b'], 'L0_ffn_wo_w': _L0_ffn_in['wo_w'], 'L0_ffn_wo_b': _L0_ffn_in['wo_b']}

def reference(x, x_txt, L0_tok_W0, L0_tok_as0, L0_tok_ad0, L0_tok_bg0, L0_tok_R0, L0_tok_g0, L0_tok_b0, L0_tok_W1, L0_tok_as1, L0_tok_ad1, L0_tok_bg1, L0_tok_R1, L0_tok_g1, L0_tok_b1, L0_tok_W2, L0_tok_as2, L0_tok_ad2, L0_tok_bg2, L0_tok_R2, L0_tok_g2, L0_tok_b2, L0_tok_fpW, L0_tok_fpb, L0_tok_fng, L0_tok_fnb, L0_tok_edge_index, L0_txt_conv_w, L0_attn_in_proj_w, L0_attn_conv_w, L0_attn_conv_b, L0_attn_x_proj_w, L0_attn_dt_w, L0_attn_dt_b, L0_attn_A_log, L0_attn_D_param, L0_attn_out_w, L0_attn_ln_g, L0_attn_ln_b, L0_ffn_pos_w, L0_ffn_pos_b, L0_ffn_qkv_w, L0_ffn_qkv_b, L0_ffn_wo_w, L0_ffn_wo_b):
    import jax
    import jax.numpy as jnp

    def _L0_tok_ref(pose_seq, W0, as0, ad0, bg0, R0, g0, b0, W1, as1, ad1, bg1, R1, g1, b1, W2, as2, ad2, bg2, R2, g2, b2, fpW, fpb, fng, fnb, edge_index):
        import jax, jax.numpy as jnp
        import numpy as np
        J = 50
        HEADS = 4
        DIMS = [3, 64, 128, 64]
        POSE_DIM = 128
        B, T = (16, 128)

        def build_edge_index():
            e = []
            for i in range(J - 1):
                e.append((i, i + 1))
                e.append((i + 1, i))
            for i in range(J):
                e.append((i, i))
            e = sorted(e)
            return jnp.array(e, dtype=jnp.int32).T

        def _layer_norm(x, g, b, eps=1e-05):
            mu = jnp.mean(x, axis=-1, keepdims=True)
            var = jnp.mean(jnp.square(x - mu), axis=-1, keepdims=True)
            return (x - mu) * jax.lax.rsqrt(var + eps) * g + b

        def _gat(x, src, dst, W, a_s, a_d, bias):
            G, Jn, _ = x.shape
            H, C = a_s.shape
            h = (x @ W).reshape(G, Jn, H, C)
            es = jnp.einsum('gjhc,hc->gjh', h, a_s)[:, src]
            ed = jnp.einsum('gjhc,hc->gjh', h, a_d)[:, dst]
            e = jax.nn.leaky_relu(es + ed, 0.2)
            m = jnp.full((G, Jn, H), -jnp.inf, e.dtype).at[:, dst].max(e)
            m = jax.lax.stop_gradient(m)
            w = jnp.exp(e - m[:, dst])
            den = jnp.zeros((G, Jn, H), e.dtype).at[:, dst].add(w)
            alpha = w / den[:, dst]
            out = jnp.zeros((G, Jn, H, C), e.dtype).at[:, dst].add(alpha[..., None] * h[:, src])
            return out.reshape(G, Jn, H * C) + bias

        def _forward(pose_seq, layers, fpW, fpb, fng, fnb, edge_index):
            Bb, Tt = (pose_seq.shape[0], pose_seq.shape[1])
            x = pose_seq.reshape(Bb * Tt, J, 3)
            src, dst = (edge_index[0], edge_index[1])
            for W, a_s, a_d, bg, R, g, b in layers:
                h = _gat(x, src, dst, W, a_s, a_d, bg)
                res = x @ R
                x = jax.nn.gelu(_layer_norm(h + res, g, b), approximate=False)
            x = x.reshape(Bb * Tt, J * DIMS[-1]) @ fpW + fpb
            x = _layer_norm(x, fng, fnb)
            return x.reshape(Bb, Tt, POSE_DIM)
        layers = [(W0, as0, ad0, bg0, R0, g0, b0), (W1, as1, ad1, bg1, R1, g1, b1), (W2, as2, ad2, bg2, R2, g2, b2)]
        return _forward(pose_seq, layers, fpW, fpb, fng, fnb, edge_index)

    def _L0_txt_ref(token_ids, conv_w):
        import jax, jax.numpy as jnp
        import numpy as np
        VOCAB = 8000
        EMB = 128
        K = 3
        B, T = (8, 1024)
        'Equivalent to one_hot(token_ids) -> Conv1d(V->F, k=K, pad=K//2, no bias).\n\n            Because the conv input is one-hot over the vocab channel, the V-dim\n            contraction reduces to gathering one weight row per (position, tap):\n              out[b,t,f] = sum_k W[f, token[b, t+k-pad], k]   (zero outside [0,T)).\n            '
        Bn, Tn = token_ids.shape
        F_, V_, Kn = conv_w.shape
        pad = Kn // 2
        out = jnp.zeros((Bn, Tn, F_), dtype=conv_w.dtype)
        t = jnp.arange(Tn)
        for k in range(Kn):
            shift = k - pad
            src = t + shift
            valid = (src >= 0) & (src < Tn)
            src_c = jnp.clip(src, 0, Tn - 1)
            ids = token_ids[:, src_c]
            table_k = conv_w[:, :, k].T
            emb = table_k[ids]
            out = out + jnp.where(valid[None, :, None], emb, jnp.zeros((), conv_w.dtype))
        return out

    def _L0_attn_ref(x, in_proj_w, conv_w, conv_b, x_proj_w, dt_w, dt_b, A_log, D_param, out_w, ln_g, ln_b):
        import jax, jax.numpy as jnp
        import numpy as np
        L = 4
        D_MODEL = 128
        D_INNER = 256
        D_STATE = 64
        D_CONV = 4
        BATCH = 64
        SEQ = 117

        def _layer_norm(v, g, b, eps=1e-05):
            mu = v.mean(-1, keepdims=True)
            var = ((v - mu) ** 2).mean(-1, keepdims=True)
            return (v - mu) / jnp.sqrt(var + eps) * g + b

        def _mamba_block(x, in_w, cw, cb, xw, dw, db, alog, dvec, ow, g, b):
            xz = x @ in_w
            xm, z = jnp.split(xz, 2, axis=-1)
            lhs = xm.transpose(0, 2, 1)
            conv = jax.lax.conv_general_dilated(lhs, cw, window_strides=(1,), padding=[(D_CONV - 1, 0)], dimension_numbers=('NCH', 'OIH', 'NCH'), feature_group_count=D_INNER)
            xc = jax.nn.silu(conv.transpose(0, 2, 1) + cb)
            Bp, Cp = jnp.split(xc @ xw, 2, axis=-1)
            dt = jax.nn.softplus(xc @ dw + db)
            A = -jnp.exp(alog)

            def step(h, inp):
                xt, dtt, Bt, Ct = inp
                h = jnp.exp(dtt[..., None] * A) * h + (dtt * xt)[..., None] * Bt[:, None, :]
                y = jnp.einsum('bdn,bn->bd', h, Ct) + dvec * xt
                return (h, y)
            h0 = jnp.zeros((x.shape[0], D_INNER, D_STATE), x.dtype)
            xs = (xc.transpose(1, 0, 2), dt.transpose(1, 0, 2), Bp.transpose(1, 0, 2), Cp.transpose(1, 0, 2))
            _, ys = jax.lax.scan(step, h0, xs)
            y = ys.transpose(1, 0, 2) * jax.nn.silu(z)
            out = y @ ow
            return _layer_norm(out + x, g, b)
        for i in range(L):
            x = _mamba_block(x, in_proj_w[i], conv_w[i], conv_b[i], x_proj_w[i], dt_w[i], dt_b[i], A_log[i], D_param[i], out_w[i], ln_g[i], ln_b[i])
        return x

    def _L0_ffn_ref(x, pos_w, pos_b, qkv_w, qkv_b, wo_w, wo_b):
        import jax, jax.numpy as jnp
        import numpy as np
        from jax import lax
        N, M, DIM, HEADS, TOPK = (4, 512, 128, 8, 16)

        def _split_heads(t, h):
            n, m, c = t.shape
            return t.reshape(n, m, h, c // h).transpose(0, 2, 1, 3).reshape(n * h, m, c // h)
        n, m, c = x.shape
        h = HEADS
        scale = c ** (-0.5)
        pos = lax.conv_general_dilated(x.transpose(0, 2, 1), pos_w, window_strides=(1,), padding=[(1, 1)], feature_group_count=c, dimension_numbers=('NCH', 'OIH', 'NCH'))
        x = x + (pos + pos_b[None, :, None]).transpose(0, 2, 1)
        qkv = x @ qkv_w.T + qkv_b
        q, k, v = jnp.split(qkv, [c, 2 * c], axis=-1)
        q = _split_heads(q, h)
        k = _split_heads(k, h)
        v = _split_heads(v, h)
        qd = lax.stop_gradient(q)
        kd = lax.stop_gradient(k)
        logits = jnp.einsum('bmd,bpd->bmp', qd * scale, kd)
        _, idx = lax.top_k(logits, TOPK)
        gather = jax.vmap(lambda t, i: t[i])
        k_sel = gather(k, idx)
        v_sel = gather(v, idx)
        attn = jax.nn.softmax(jnp.einsum('bmd,bmkd->bmk', q * scale, k_sel), axis=-1)
        out = jnp.einsum('bmk,bmkd->bmd', attn, v_sel)
        d = c // h
        out = out.reshape(n, h, m, d).transpose(0, 2, 1, 3).reshape(n, m, c)
        return out @ wo_w.T + wo_b
    h = _L0_tok_ref(x, L0_tok_W0, L0_tok_as0, L0_tok_ad0, L0_tok_bg0, L0_tok_R0, L0_tok_g0, L0_tok_b0, L0_tok_W1, L0_tok_as1, L0_tok_ad1, L0_tok_bg1, L0_tok_R1, L0_tok_g1, L0_tok_b1, L0_tok_W2, L0_tok_as2, L0_tok_ad2, L0_tok_bg2, L0_tok_R2, L0_tok_g2, L0_tok_b2, L0_tok_fpW, L0_tok_fpb, L0_tok_fng, L0_tok_fnb, L0_tok_edge_index)
    h = jnp.concatenate([h, _L0_txt_ref(x_txt, L0_txt_conv_w)], axis=1)
    h = h + _L0_attn_ref(_layernorm(h, axis=-1), L0_attn_in_proj_w, L0_attn_conv_w, L0_attn_conv_b, L0_attn_x_proj_w, L0_attn_dt_w, L0_attn_dt_b, L0_attn_A_log, L0_attn_D_param, L0_attn_out_w, L0_attn_ln_g, L0_attn_ln_b)
    h = h + _L0_ffn_ref(_layernorm(h, axis=-1), L0_ffn_pos_w, L0_ffn_pos_b, L0_ffn_qkv_w, L0_ffn_qkv_b, L0_ffn_wo_w, L0_ffn_wo_b)
    return h

_drawn_inputs = setup_inputs


def setup_inputs(seed=0):
    import zlib

    import numpy as np

    out = dict(_drawn_inputs(seed))
    spreads = {'L0_tok_bg0': (0.0, 0.1),
     'L0_tok_g0': (1.0, 0.2),
     'L0_tok_b0': (0.0, 0.1),
     'L0_tok_bg1': (0.0, 0.1),
     'L0_tok_g1': (1.0, 0.2),
     'L0_tok_b1': (0.0, 0.1),
     'L0_tok_bg2': (0.0, 0.1),
     'L0_tok_g2': (1.0, 0.2),
     'L0_tok_b2': (0.0, 0.1),
     'L0_tok_fpb': (0.0, 0.1),
     'L0_tok_fng': (1.0, 0.2),
     'L0_tok_fnb': (0.0, 0.1),
     'L0_attn_conv_b': (0.0, 0.8),
     'L0_attn_dt_b': (-1.0, 0.6),
     'L0_attn_D_param': (1.0, 0.6),
     'L0_attn_ln_g': (1.0, 0.2),
     'L0_attn_ln_b': (0.0, 0.1)}
    factors = {'L0_tok_ad2': 5.093,
     'L0_attn_in_proj_w': 8.0,
     'L0_attn_conv_w': 8.0,
     'L0_attn_x_proj_w': 8.0,
     'L0_attn_dt_w': 8.0,
     'L0_attn_A_log': 8.0,
     'L0_attn_out_w': 8.0,
     'L0_ffn_pos_w': 8.0,
     'L0_ffn_pos_b': 8.0,
     'L0_ffn_qkv_w': 3.509,
     'L0_ffn_qkv_b': 8.0,
     'L0_ffn_wo_w': 3.333,
     'L0_ffn_wo_b': 3.515}
    for name, (base, spread) in spreads.items():
        noise = np.random.default_rng([zlib.crc32(name.encode()), seed]).standard_normal(out[name].shape)
        drawn = base * np.exp(spread * noise) if base else spread * noise
        out[name] = jnp.asarray(drawn.astype(out[name].dtype))
    for name, factor in factors.items():
        out[name] = (out[name] * factor).astype(out[name].dtype)
    return out
```

```python
from contextlib import ExitStack

import numpy as np

import concourse.bass as bass
from concourse import mybir

F32 = mybir.dt.float32
BF16 = mybir.dt.bfloat16
I32 = mybir.dt.int32
ALU = mybir.AluOpType
ACT = mybir.ActivationFunctionType
AX = mybir.AxisListType

P = 128
EPS = 1e-5
B, S = 4, 640
TILES = S // P


def embed_stage(nc, T, shared):
    h_tok, x_tok, ident = shared["h_tok"], shared["x_tok"], shared["ident"]
    DM = h_tok.shape[2]
    J = T["xT"].shape[2]
    NE = T["edges"].shape[1]
    H = 4
    CIN = [T["W"][l].shape[0] for l in range(3)]
    COUT = [T["W"][l].shape[1] for l in range(3)]
    VOCAB = T["table"].shape[0] // 3
    NT = (TILES - 1) * B
    PB = B // 2
    GR, BLK = J // 2, 25
    NB = GR // BLK
    NG = 2 * GR
    RING = 4
    EDGES = 37
    LOAD = 19
    E1, E2 = P, NE - P
    KEY = 256.0
    LOW = -3.0e38
    assert J % 2 == 0 and GR % BLK == 0 and NE % EDGES == 0 and P < NE <= KEY and 2 * J <= P

    with ExitStack() as ctx:
        def sb(name, shape, dt=F32):
            return ctx.enter_context(nc.sbuf_tensor("g_" + name, shape, dt))

        def ps(name, shape):
            return ctx.enter_context(nc.psum_tensor("g_" + name, shape, F32))

        def sem(name):
            return ctx.enter_context(nc.semaphore("g_" + name))

        ids = sb("ids", [P, 3, NT], I32)
        after = sb("after", [P, NT, DM])
        E = sb("E", [P, 2, H, NE])
        F = sb("F", [P, 2 * H * NE])
        M = sb("M", [P, 2 * H * NE])
        Ef = E[:].rearrange("p b h e -> p (b h e)")

        def at(home, first, *shape):
            size = int(np.prod(shape))
            names = "abc"[:len(shape)]
            part = home[:, first:first + size]
            if len(shape) == 1:
                return part
            return part.rearrange(f"p ({' '.join(names)}) -> p {' '.join(names)}", **dict(zip(names, shape)))

        ei_row = at(Ef, 0, 2, NE).bitcast(I32)
        ei_col = sb("ei_col", [P, 2, 2], I32)
        row = at(Ef, 2 * NE, 2, NE)
        col = sb("col", [P, 2, 2])
        iota_i = at(Ef, 4 * NE, NE).bitcast(I32)
        key_r = at(Ef, 5 * NE, NE)
        iota_r = at(F, 0, NE)
        perm = at(F, NE, 2, NE)
        colb = at(F, 3 * NE, 2, 2, P)
        avec = at(M, 0, 3, 2, P)
        awork = at(M, 6 * P, P)
        iota_pi = sb("iota_pi", [P, 2], I32)
        iota_p = sb("iota_p", [P, 2])
        key_c = sb("key_c", [P, 2])
        rank = sb("rank", [P, 2])
        srt = sb("srt", [P, 2, NE])
        srt_i = sb("srt_i", [1, 2, NE], I32)
        hot = sb("hot", [P, 2, NE])
        keepf = sb("keepf", [P, H, NE])
        resetf = sb("resetf", [P, H, NE])
        keepr = sb("keepr", [P, H, NE])
        isend = sb("isend", [P, NE])
        wc = [sb(f"wc{l}", [(3, P, P)[l], 2 * COUT[l] + 2 * H]) for l in range(3)]
        bgb = sb("bgb", [P, 3, P])
        gcol = sb("gcol", [P, 3])
        bcol = sb("bcol", [P, 3])
        fpb = sb("fpb", [1, DM])
        ones = sb("ones", [1, P])
        fng = sb("fng", [P, DM])
        fnb = sb("fnb", [P, DM])
        accA = sb("accA", [P, 2 * J, 64])
        accB = sb("accB", [P, 2 * J, 128])
        hbuf = sb("hbuf", [P, 2 * J * 128])
        acc = [accA, accB, accA]
        hb = [hbuf[:, 0:2 * J * COUT[l]].rearrange("p (b j c) -> p b j c", b=2, c=COUT[l]) for l in range(3)]
        fpw = hbuf[:, 2 * J * 64:2 * J * 64 + GR * DM].rearrange("p (g n) -> p g n", n=DM)
        x0T = accB[0:3].rearrange("p (b j) c -> p b j c", b=2)
        esd = sb("esd", [P, 2, H, 2 * J])
        esT = sb("esT", [P, 2, H * P])
        prod = sb("prod", [P, RING, 2, 128])
        stats = sb("stats", [P, 2 * J, 6])
        mean = sb("mean", [P, 2 * J])
        rstd = sb("rstd", [P, 2 * J])
        dif = sb("dif", [P, 2 * J])
        nrm = sb("nrm", [P, 2, 2 * 128])
        xTs = sb("xTs", [P, 2, 2 * P])
        st2 = sb("st2", [P, B * TILES, 6])
        mv2 = sb("mv2", [P, B * TILES, 2])
        rs2 = sb("rs2", [P, B * TILES])

        TB = [ps(f"TB{r}", [P, 512]) for r in range(2)]
        PJ = [ps(f"PJ{r}", [P, 2, 512]) for r in range(2)]
        FP = ps("FP", [P, 512])
        SR = ps("SR", [P, 512])

        loaded, cleared = sem("loaded"), sem("cleared")
        ids_loaded, ids_ready, rows_loaded = sem("ids_loaded"), sem("ids_ready"), sem("rows_loaded")
        x_loaded, fpw_loaded = sem("x_loaded"), sem("fpw_loaded")
        iota_ready, set_dve, set_pe = sem("iota_ready"), sem("set_dve"), sem("set_pe")
        setup, perm_ready = sem("setup"), sem("perm_ready")
        nrm_ready, tr_ready, xT_ready, proj_ready = sem("nrm_ready"), sem("tr_ready"), sem("xT_ready"), sem("proj_ready")
        h_copied, acc_ready = sem("h_copied"), sem("acc_ready")
        sm_pe, sm_act, sm_dve = sem("sm_pe"), sem("sm_act"), sem("sm_dve")
        prod_ready, added = sem("prod_ready"), sem("added")
        rows_done = sem("rows_done")
        st_dve, st_act = sem("st_dve"), sem("st_act")
        fp_ready, hv_ready = sem("fp_ready"), sem("hv_ready")
        end_dve, end_act = sem("end_dve"), sem("end_act")
        waits_met = sem("waits_met")
        N_SM, N_ST = 10, 6

        def apart(eng):
            eng.sem_inc(waits_met, 1)

        def back(g):
            return 1 if g == 0 else 2

        def in_turn(eng, first, second):
            for g in range(BLK + 1):
                if g < BLK:
                    first(g)
                if g >= 1:
                    second(g - 1)

        NLOAD = 34

        with nc.Block() as block:
            @block.sync
            def _(sp):
                ids_v = ids[:].rearrange("p k (b j) -> p k b j", b=B)
                src = T["ids"].rearrange("p (b j) -> p b j", b=B)
                JJ = TILES - 1
                sp.wait_ge(cleared, 3)
                sp.dma_start(ids_v[:, 1], src).then_inc(ids_loaded, 16)
                sp.dma_start(ids_v[1:P, 0], src[0:P - 1]).then_inc(ids_loaded, 16)
                sp.dma_start(ids_v[0:1, 0, :, 1:JJ], src[P - 1:P, :, 0:JJ - 1]).then_inc(ids_loaded, 16)
                sp.dma_start(ids_v[0:P - 1, 2], src[1:P]).then_inc(ids_loaded, 16)
                sp.dma_start(ids_v[P - 1:P, 2, :, 0:JJ - 1], src[0:1, :, 1:JJ]).then_inc(ids_loaded, 16)
                loads = [(ei_row[:], T["edges"].unsqueeze(0).to_broadcast([P, 2, NE])),
                         (ei_col[:, 0, :], T["edgesT"][0:E1, :]), (ei_col[0:E2, 1, :], T["edgesT"][E1:NE, :])]
                for l in range(3):
                    n = COUT[l]
                    for k in range(2 if l == 1 else 1):
                        at = slice(64 * k, 64 * k + CIN[l])
                        loads += [(wc[l][at, 0:n], T["W"][l]), (wc[l][at, n:2 * n], T["R"][l])]
                    loads += [(avec[:, l, 0, 0:n], T["as"][l].unsqueeze(0).to_broadcast([P, n])),
                              (avec[:, l, 1, 0:n], T["ad"][l].unsqueeze(0).to_broadcast([P, n])),
                              (bgb[:, l, 0:n], T["bg"][l].unsqueeze(0).to_broadcast([P, n]))]
                    for k in range(P // n):
                        loads += [(gcol[n * k:n * k + n, l:l + 1], T["g"][l].unsqueeze(1)),
                                  (bcol[n * k:n * k + n, l:l + 1], T["b"][l].unsqueeze(1))]
                loads += [(fpb[:], T["fpb"].unsqueeze(0)), (fng[:], T["fng"].unsqueeze(0).to_broadcast([P, DM])),
                          (fnb[:], T["fnb"].unsqueeze(0).to_broadcast([P, DM]))]
                assert len(loads) == NLOAD - 1, len(loads)
                for dst, s in loads:
                    sp.dma_start(dst, s).then_inc(loaded, 16)
                with sp.Fori(0, PB) as pb:
                    sp.wait_ge(nrm_ready, pb * (3 * NG) + 1)
                    apart(sp)
                    sp.dma_start(x0T, T["xT"][:, bass.ds(pb * 2, 2)]).then_inc(x_loaded, 16)
                    sp.wait_ge(added, pb * (3 * NE) + (2 * NE + RING))
                    apart(sp)
                    sp.dma_start(fpw, T["fpW"].rearrange("(g p) n -> p g n", p=P)).then_inc(fpw_loaded, 16)

            @block.gpsimd
            def _(pool):
                pool.memset(ids[:], 4 * VOCAB).then_inc(cleared, 1)
                pool.memset(x_tok[:], 0.0).then_inc(cleared, 1)
                pool.memset(after[:], 0.0).then_inc(cleared, 1)
                pool.iota(iota_i[:], [[1, NE]], base=0, channel_multiplier=0).then_inc(iota_ready, 1)
                pool.iota(iota_pi[:, 0:1], [[0, 1]], base=0, channel_multiplier=1).then_inc(iota_ready, 1)
                pool.iota(iota_pi[:, 1:2], [[0, 1]], base=-J, channel_multiplier=1).then_inc(iota_ready, 1)
                pool.memset(ones[:], 1.0).then_inc(iota_ready, 1)
                pool.wait_ge(cleared, 3)
                pool.wait_ge(ids_ready, 2)
                for k, dst in ((1, h_tok), (0, x_tok), (2, after)):
                    for n in range(NT):
                        at = n // (TILES - 1) * TILES + 1 + n % (TILES - 1) if k < 2 else n
                        pool.indirect_dma_start(out=dst[:, at, :], out_offset=None, in_=T["table"],
                                                in_offset=bass.IndirectOffsetOnAxis(ap=ids[:, k, n:n + 1], axis=0),
                                                bounds_check=3 * VOCAB - 1, oob_is_err=False
                                                ).then_inc(rows_loaded, 16)
                src = [pool.alloc_register(f"g_src{q}") for q in range(EDGES)]
                pool.wait_ge(set_dve, 1)
                with pool.Fori(0, PB) as pb:
                    for l in range(3):
                        lp = pb * 3 + l
                        pool.wait_ge(sm_dve, lp * N_SM + N_SM)
                        apart(pool)
                        with pool.Fori(0, NE // EDGES) as i:
                            for a in range(0, EDGES, LOAD):
                                w = min(LOAD, EDGES - a)
                                pool.load(src[a:a + w], srt_i[0:1, 0, bass.ds(i * EDGES + a, w)])
                            for q in range(EDGES):
                                j = pool.snap(src[q], min_val=0, max_val=J - 1)
                                last = q - RING if q >= RING else (EDGES - 1 - q) // RING * RING + q - EDGES
                                pool.wait_ge(added, lp * NE + i * EDGES + last + 1 + RING)
                                C = COUT[l] // H
                                pool.tensor_tensor(
                                    prod[:, q % RING, :, 0:COUT[l]].rearrange("p b (h c) -> p b h c", c=C),
                                    hb[l][:, :, bass.ds(j, 1), :].rearrange("p b o (h c) -> p b (o h) c", c=C),
                                    E[:, :, :, bass.ds(i * EDGES + q, 1)].to_broadcast([P, 2, H, C]),
                                    ALU.mult).then_inc(prod_ready, 1)

            @block.scalar
            def _(act):
                act.sem_inc(xT_ready, 1)
                act.wait_ge(loaded, (NLOAD - 1) * 16)

                with act.Fori(0, PB) as pb:
                    for l in range(4):
                        n = COUT[min(l, 2)]
                        if l == 0:
                            act.wait_ge(x_loaded, pb * 16 + 16)
                        for bb in range(2):
                            with act.Fori(0, NB) as i:
                                def stage(g):
                                    r = g % 2
                                    g0 = bb * GR + g + 1 - back(g)
                                    act.wait_ge(proj_ready, (pb * 4 + l) * NG + i * BLK + g0 + 1)
                                    if l == 0:
                                        act.copy(xTs[0:3, r, :].rearrange("p (j t) -> p j t", j=2),
                                                 x0T[:, bb, bass.ds(i * (2 * BLK) + 2 * g, 2), :]).then_inc(xT_ready, 1)
                                    else:
                                        act.wait_ge(tr_ready, (pb * 3 + (l - 1)) * NG + i * BLK + (bb * GR + g + 1) + 1)
                                        w = 2 * P if COUT[l - 1] == P else P
                                        act.activation(xTs[:, r, 0:w], TB[r][:, 0:w], ACT.Gelu,
                                                       scale=gcol[:, l - 1:l], bias=bcol[:, l - 1:l]).then_inc(xT_ready, 1)

                                def take(g):
                                    if l == 3:
                                        return
                                    r = g % 2
                                    act.wait_ge(proj_ready, (pb * 4 + l) * NG + i * BLK + (bb * GR + g + 1) + 1)
                                    act.copy(hb[l][:, bb, bass.ds(i * (2 * BLK) + 2 * g, 2), :], PJ[r][:, :, 0:n]
                                             ).then_inc(h_copied, 1)

                                in_turn(act, stage, take)
                        if l == 3:
                            continue
                        S0 = (pb * 3 + l) * 3
                        act.wait_ge(sm_pe, (pb * 3 + l) * 2 + 1)
                        for bb in range(2):
                            ins = act.copy(esT[0:2 * J, bb, :], TB[bb][0:2 * J, :])
                        ins.then_inc(sm_act, 1)
                        act.wait_ge(sm_pe, (pb * 3 + l) * 2 + 2)
                        for bb in range(2):
                            ins = act.copy(E[:, bb].rearrange("p (a h) e -> p a (h e)", a=2), PJ[bb][:, :, 0:2 * NE])
                        ins.then_inc(sm_act, 1)
                        act.wait_ge(sm_dve, (pb * 3 + l) * N_SM + 5)
                        act.activation(Ef, Ef, ACT.Exp).then_inc(sm_act, 1)
                        act.wait_ge(st_dve, (pb * 3 + l) * N_ST + 5)
                        act.activation(rstd[:], rstd[:], ACT.Sqrt).then_inc(st_act, 1)
                act.wait_ge(end_dve, 3)
                act.activation(rs2[:, 0:B], mv2[:, 0:B, 1], ACT.Sqrt).then_inc(end_act, 1)
                act.wait_ge(end_dve, 12)
                act.activation(rs2[:], mv2[:, :, 1], ACT.Sqrt).then_inc(end_act, 1)

            @block.tensor
            def _(pe):
                pe.sem_inc(tr_ready, 1)
                pe.sem_inc(proj_ready, 1)
                pe.wait_ge(perm_ready, 1)
                for k in range(2):
                    pe.matmul(SR[:, k * NE:(k + 1) * NE], colb[:, 0, k, :], perm[:, 0, :], start=True, stop=False)
                    ins = pe.matmul(SR[:, k * NE:(k + 1) * NE], colb[0:E2, 1, k, :], perm[0:E2, 1, :], start=False, stop=True)
                ins.then_inc(set_pe, 1)
                pe.wait_ge(set_dve, 1)
                with pe.Fori(0, PB) as pb:
                    for l in range(4):
                        n = COUT[min(l, 2)]
                        if l == 3:
                            pe.wait_ge(fpw_loaded, pb * 16 + 16)
                        for bb in range(2):
                            if l == 3:
                                pe.wait_ge(hv_ready, pb * 2 + bb + 1)
                                pe.matmul(FP[:, 0:DM], ones[:], fpb[:], start=True, stop=False, skip_group_check=True)
                            with pe.Fori(0, NB) as i:
                                def turn(g):
                                    if l == 0:
                                        return
                                    r = g % 2
                                    N = (pb * 3 + (l - 1)) * NG + i * BLK + (bb * GR + g)
                                    pe.wait_ge(nrm_ready, N + 1 + 1)
                                    pe.wait_ge(xT_ready, (pb * 4 + l) * NG + i * BLK + (bb * GR + g + 1 - back(g)) + 1)
                                    if COUT[l - 1] == P:
                                        for a in range(2):
                                            ins = pe.transpose(TB[r][:, a * P:(a + 1) * P], nrm[:, r, a * P:(a + 1) * P], ident[:])
                                    else:
                                        ins = pe.transpose(TB[r][:, 0:P], nrm[:, r, 0:P], ident[:])
                                    ins.then_inc(tr_ready, 1)

                                def project(g):
                                    r = g % 2
                                    G = (pb * 4 + l) * NG + i * BLK + (bb * GR + g)
                                    pe.wait_ge(xT_ready, G + 1 + 1)
                                    if l == 3:
                                        pe.matmul(FP[:, 0:DM], xTs[:, r, 0:P], fpw[:, bass.ds(i * BLK + g, 1), :].rearrange("p o n -> p (o n)"),
                                                  start=False, stop=False, skip_group_check=True).then_inc(proj_ready, 1)
                                        return
                                    pe.wait_ge(acc_ready, (pb * 3 + l) * NG + i * BLK + (bb * GR + g + 1 - back(g)) + 1)
                                    for a in range(2):
                                        if l == 0:
                                            lhs, w = xTs[0:3, r, a * P:(a + 1) * P], wc[0][:]
                                        elif l == 1:
                                            lhs, w = xTs[64 * a:64 * a + 64, r, 0:P], wc[1][64 * a:64 * a + 64, :]
                                        else:
                                            lhs, w = xTs[:, r, a * P:(a + 1) * P], wc[2][:]
                                        ins = pe.matmul(PJ[r][:, a, 0:2 * n + 2 * H], lhs, w, start=True, stop=True)
                                    ins.then_inc(proj_ready, 1)

                                in_turn(pe, turn, project)
                            if l == 3:
                                pe.matmul(FP[0:1, DM:DM + 1], ones[:, 0:1], ones[:, 0:1], start=False, stop=False,
                                          skip_group_check=True).then_inc(fp_ready, 1)
                        if l == 3:
                            continue
                        lp = pb * 3 + l
                        pe.wait_ge(acc_ready, lp * NG + NG + 1)
                        for bb in range(2):
                            for hd in range(H):
                                ins = pe.transpose(TB[bb][0:2 * J, hd * P:(hd + 1) * P], esd[:, bb, hd, :], ident[:])
                        ins.then_inc(sm_pe, 1)
                        pe.wait_ge(sm_act, lp * 3 + 1)
                        for bb in range(2):
                            for hd in range(H):
                                ins = pe.matmul(PJ[bb][:, hd // 2, hd % 2 * NE:(hd % 2 + 1) * NE],
                                                esT[0:2 * J, bb, hd * P:(hd + 1) * P], hot[0:2 * J, 0, :],
                                                start=True, stop=True)
                        ins.then_inc(sm_pe, 1)

            @block.vector
            def _(v):
                v.sem_inc(acc_ready, 1)
                v.sem_inc(nrm_ready, 1)
                v.sem_inc(hv_ready, 1)
                done = [0]

                def chain(ins):
                    ins.then_inc(setup, 1)
                    done[0] += 1
                    v.wait_ge(setup, done[0])

                v.wait_ge(ids_loaded, 5 * 16)
                v.tensor_scalar(ids[:, 1, :], ids[:, 1, :], float(VOCAB), None, ALU.add).then_inc(ids_ready, 1)
                v.tensor_scalar(ids[:, 2, :], ids[:, 2, :], float(2 * VOCAB), None, ALU.add).then_inc(ids_ready, 1)
                v.wait_ge(loaded, (NLOAD - 1) * 16)
                v.wait_ge(iota_ready, 4)
                v.tensor_copy(iota_r[:], iota_i[:])
                v.tensor_copy(iota_p[:], iota_pi[:])
                v.tensor_copy(row[:], ei_row[:])
                v.tensor_copy(col[:, 0, :], ei_col[:, 0, :])
                chain(v.tensor_copy(col[0:E2, 1, :], ei_col[0:E2, 1, :]))
                v.scalar_tensor_tensor(key_r[:], row[:, 1, :], KEY, iota_r[:], ALU.mult, ALU.add)
                v.scalar_tensor_tensor(key_c[:, 0:1], col[:, 0, 1:2], KEY, iota_p[:, 0:1], ALU.mult, ALU.add)
                chain(v.scalar_tensor_tensor(key_c[0:E2, 1:2], col[0:E2, 1, 1:2], KEY, iota_p[0:E2, 0:1], ALU.mult, ALU.add))
                chain(v.tensor_scalar(key_c[0:E2, 1:2], key_c[0:E2, 1:2], float(E1), None, ALU.add))
                chain(v.tensor_scalar(perm[:, 0, :], key_r[:], key_c[:, 0:1], 0.0, ALU.is_lt, ALU.add, accum_out=rank[:, 0:1]))
                chain(v.tensor_scalar(perm[0:E2, 1, :], key_r[0:E2], key_c[0:E2, 1:2], 0.0, ALU.is_lt, ALU.add,
                                      accum_out=rank[0:E2, 1:2]))
                v.tensor_scalar(perm[:, 0, :], iota_r[:], rank[:, 0:1], None, ALU.is_equal)
                v.tensor_scalar(perm[0:E2, 1, :], iota_r[0:E2], rank[0:E2, 1:2], None, ALU.is_equal)
                v.tensor_copy(colb[:, 0], col[:, 0, :].unsqueeze(2).to_broadcast([P, 2, P]))
                v.tensor_copy(colb[0:E2, 1], col[0:E2, 1, :].unsqueeze(2).to_broadcast([E2, 2, P])).then_inc(perm_ready, 1)
                v.wait_ge(set_pe, 1)
                chain(v.tensor_copy(srt[:].rearrange("p k e -> p (k e)"), SR[:, 0:2 * NE]))
                v.tensor_copy(srt_i[:], srt[0:1])
                v.tensor_scalar(hot[:, 0, :], srt[:, 0, :], iota_p[:, 0:1], None, ALU.is_equal)
                chain(v.tensor_scalar(hot[:, 1, :], srt[:, 1, :], iota_p[:, 1:2], None, ALU.is_equal))
                chain(v.tensor_tensor(hot[:, 0, :], hot[:, 0, :], hot[:, 1, :], ALU.add))
                chain(v.memset(keepf[:], 0.0))
                chain(v.memset(keepr[:], 0.0))
                same = [srt[:, 1, 1:NE].unsqueeze(1).to_broadcast([P, H, NE - 1]),
                        srt[:, 1, 0:NE - 1].unsqueeze(1).to_broadcast([P, H, NE - 1])]
                v.tensor_tensor(keepf[:, :, 1:NE], same[0], same[1], ALU.is_equal)
                chain(v.tensor_tensor(keepr[:, :, 0:NE - 1], same[0], same[1], ALU.is_equal))
                v.tensor_scalar(resetf[:], keepf[:], -1.0, -LOW, ALU.add, ALU.mult)
                chain(v.tensor_scalar(isend[:], keepr[:, 0, :], -1.0, 1.0, ALU.mult, ALU.add))
                for l in range(3):
                    n, k = COUT[l], 3 if l == 0 else P
                    for s in range(2):
                        chain(v.tensor_tensor(awork[0:k, 0:n], wc[l][:, 0:n], avec[0:k, l, s, 0:n], ALU.mult))
                        chain(v.tensor_reduce(wc[l][:, 2 * n + s * H:2 * n + (s + 1) * H],
                                              awork[0:k, 0:n].rearrange("p (h c) -> p h c", h=H), AX.X, ALU.add))
                for q in range(RING):
                    ins = v.memset(prod[:, q, :, 0:8], 0.0).then_inc(added, 1)
                v.wait_ge(added, RING)
                v.memset(dif[:], 0.0).then_inc(set_dve, 1)
                v.wait_ge(set_dve, 1)

                dst = [v.alloc_register(f"g_dst{q}") for q in range(EDGES)]
                keepf_f = keepf[:].rearrange("p h e -> p (h e)")
                resetf_f = resetf[:].rearrange("p h e -> p (h e)")
                keepr_f = keepr[:].rearrange("p h e -> p (h e)")
                F3 = F[:].rearrange("p (h e) -> p h e", e=NE)
                isend3 = isend[:].unsqueeze(1).to_broadcast([P, 2 * H, NE])

                def scan(to, keep, of, op0, op1, step=1):
                    for bb in range(2):
                        a, b = bb * H * NE, (bb + 1) * H * NE
                        ins = v.tensor_tensor_scan(to[:, a:b][:, ::step], keep[:, ::step], of[:, a:b][:, ::step], 0.0, op0, op1)
                    return ins

                with v.Fori(0, PB) as pb:
                    for l in range(4):
                        n = COUT[min(l, 2)]
                        m = COUT[l - 1] if l else 0
                        for bb in range(2):
                            with v.Fori(0, NB) as i:
                                def normalise(g):
                                    if l == 0:
                                        return
                                    r = g % 2
                                    v.wait_ge(tr_ready, (pb * 3 + (l - 1)) * NG + i * BLK + (bb * GR + g + 1 - back(g)) + 1)
                                    for a in range(2):
                                        nd = i * (2 * BLK) + (bb * J + 2 * g + a)
                                        ins = v.tensor_scalar(nrm[:, r, a * m:(a + 1) * m],
                                                              acc[l - 1][:, bass.ds(nd, 1), :].rearrange("p o c -> p (o c)"),
                                                              mean[:, bass.ds(nd, 1)], rstd[:, bass.ds(nd, 1)],
                                                              ALU.subtract, ALU.mult)
                                    ins.then_inc(nrm_ready, 1)

                                def take(g):
                                    if l == 3:
                                        return
                                    r = g % 2
                                    G = (pb * 3 + l) * NG + i * BLK + (bb * GR + g)
                                    v.wait_ge(h_copied, G + 1)
                                    nodes = bass.ds(i * (2 * BLK) + (bb * J + 2 * g), 2)
                                    v.tensor_tensor(acc[l][:, nodes, :], PJ[r][:, :, n:2 * n],
                                                    bgb[:, l, 0:n].unsqueeze(1).to_broadcast([P, 2, n]), ALU.add)
                                    here = bass.ds(i * (2 * BLK) + 2 * g, 2)
                                    v.tensor_copy(esd[:, bb].rearrange("p h (s j) -> p s h j", s=2)[:, :, :, here],
                                                  PJ[r][:, :, 2 * n:2 * n + 2 * H].rearrange("p j (s h) -> p s h j", s=2)
                                                  ).then_inc(acc_ready, 1)

                                in_turn(v, normalise, take)
                            if l == 3:
                                v.wait_ge(fp_ready, pb * 2 + (bb + 1))
                                v.tensor_copy(h_tok[:, bass.ds(pb * (2 * TILES) + bb * TILES, 1), :].rearrange("p o c -> p (o c)"), FP[:, 0:DM]
                                              ).then_inc(hv_ready, 1)
                        if l == 3:
                            continue
                        lp = pb * 3 + l
                        D0 = lp * N_SM
                        v.wait_ge(sm_act, lp * 3 + 2)
                        v.scalar_tensor_tensor(Ef, Ef, 0.2, Ef, ALU.mult, ALU.max).then_inc(sm_dve, 1)
                        v.wait_ge(sm_dve, D0 + 1)
                        scan(F, resetf_f, Ef, ALU.add, ALU.max).then_inc(sm_dve, 1)
                        v.wait_ge(sm_dve, D0 + 2)
                        v.tensor_tensor(F3, F3, isend3, ALU.mult).then_inc(sm_dve, 1)
                        v.wait_ge(sm_dve, D0 + 3)
                        scan(M, keepr_f, F, ALU.mult, ALU.add, -1).then_inc(sm_dve, 1)
                        v.wait_ge(sm_dve, D0 + 4)
                        v.tensor_tensor(Ef, Ef, M[:], ALU.subtract).then_inc(sm_dve, 1)
                        v.wait_ge(sm_act, lp * 3 + 3)
                        scan(F, keepf_f, Ef, ALU.mult, ALU.add).then_inc(sm_dve, 1)
                        v.wait_ge(sm_dve, D0 + 6)
                        v.tensor_tensor(F3, F3, isend3, ALU.mult).then_inc(sm_dve, 1)
                        v.wait_ge(sm_dve, D0 + 7)
                        scan(M, keepr_f, F, ALU.mult, ALU.add, -1).then_inc(sm_dve, 1)
                        v.wait_ge(sm_dve, D0 + 8)
                        v.reciprocal(M[:], M[:]).then_inc(sm_dve, 1)
                        v.wait_ge(sm_dve, D0 + 9)
                        v.tensor_tensor(Ef, Ef, M[:], ALU.mult).then_inc(sm_dve, 1)
                        av = acc[l][:].rearrange("p (b j) c -> p b j c", b=2)
                        with v.Fori(0, NE // EDGES) as i:
                            for a in range(0, EDGES, LOAD):
                                w = min(LOAD, EDGES - a)
                                v.load(dst[a:a + w], srt_i[0:1, 1, bass.ds(i * EDGES + a, w)])
                            for q in range(EDGES):
                                j = v.snap(dst[q], min_val=0, max_val=J - 1)
                                e = lp * NE + i * EDGES + q
                                v.wait_ge(prod_ready, e + 1)
                                v.wait_ge(added, e + RING)
                                to = av[:, :, bass.ds(j, 1), :].rearrange("p b o c -> p b (o c)")
                                v.tensor_tensor(to, to, prod[:, q % RING, :, 0:n], ALU.add).then_inc(added, 1)
                        v.wait_ge(added, lp * NE + NE + RING)
                        apart(v)
                        with v.Fori(0, 2 * J // 10) as i:
                            for q in range(10):
                                nd = bass.ds(i * 10 + q, 1)
                                ins = v.bn_stats(stats[:, nd, :].rearrange("p o s -> p (o s)"),
                                                 acc[l][:, nd, :].rearrange("p o c -> p (o c)"))
                            ins.then_inc(rows_done, 1)
                        Q = lp * N_ST
                        v.wait_ge(rows_done, (lp + 1) * (2 * J // 10))
                        v.tensor_tensor(mean[:], stats[:, :, 1], stats[:, :, 4], ALU.add)
                        v.tensor_tensor(dif[:], stats[:, :, 1], stats[:, :, 4], ALU.subtract)
                        v.tensor_tensor(rstd[:], stats[:, :, 2], stats[:, :, 5], ALU.add).then_inc(st_dve, 1)
                        v.wait_ge(st_dve, Q + 1)
                        v.tensor_scalar(mean[:], mean[:], 0.5, None, ALU.mult)
                        v.tensor_tensor(dif[:], dif[:], dif[:], ALU.mult).then_inc(st_dve, 1)
                        v.wait_ge(st_dve, Q + 2)
                        v.tensor_scalar(rstd[:], rstd[:], 1.0 / n, EPS, ALU.mult, ALU.add).then_inc(st_dve, 1)
                        v.wait_ge(st_dve, Q + 3)
                        v.tensor_scalar(dif[:], dif[:], 0.25, None, ALU.mult).then_inc(st_dve, 1)
                        v.wait_ge(st_dve, Q + 4)
                        v.tensor_tensor(rstd[:], rstd[:], dif[:], ALU.add).then_inc(st_dve, 1)
                        v.wait_ge(st_act, lp + 1)
                        v.reciprocal(rstd[:], rstd[:]).then_inc(st_dve, 1)
                        v.wait_ge(st_dve, Q + 6)
                        apart(v)
                ends = [0]

                def link(ins):
                    ins.then_inc(end_dve, 1)
                    ends[0] += 1
                    v.wait_ge(end_dve, ends[0])

                v.wait_ge(hv_ready, B + 1)
                hB = h_tok[:].rearrange("p (b j) c -> p b j c", b=B)
                xB = x_tok[:].rearrange("p (b j) c -> p b j c", b=B)
                hp = hB[:, :, 0, :]
                for b in range(B):
                    ins = v.bn_stats(st2[:, b, :], hp[:, b, :])
                link(ins)
                for b in range(B):
                    ins = v.bn_aggr(mv2[:, b, :], st2[:, b, :])
                link(ins)
                link(v.tensor_scalar(mv2[:, 0:B, 1], mv2[:, 0:B, 1], EPS, None, ALU.add))
                v.wait_ge(end_act, 1)
                link(v.reciprocal(rs2[:, 0:B], rs2[:, 0:B]))
                for b in range(B):
                    ins = v.tensor_scalar(hp[:, b, :], hp[:, b, :], mv2[:, b, 0:1], rs2[:, b:b + 1],
                                          ALU.subtract, ALU.mult)
                link(ins)
                link(v.tensor_tensor(hp, hp, fng[:].unsqueeze(1).to_broadcast([P, B, DM]), ALU.mult))
                link(v.tensor_tensor(hp, hp, fnb[:].unsqueeze(1).to_broadcast([P, B, DM]), ALU.add))
                v.wait_ge(rows_loaded, 3 * NT * 16)
                JJ = TILES - 1
                aB = after[:].rearrange("p (b j) c -> p b (j c)", b=B)
                hw = hB[:, :, 1:TILES, :].rearrange("p b j c -> p b (j c)")
                xw = xB[:, :, 1:TILES, :].rearrange("p b j c -> p b (j c)")
                link(v.tensor_tensor(hw, xw, hw, ALU.add))
                link(v.tensor_tensor(hw, hw, aB, ALU.add))
                for t in range(B * TILES):
                    ins = v.bn_stats(st2[:, t, :], h_tok[:, t, :])
                link(ins)
                for t in range(B * TILES):
                    ins = v.bn_aggr(mv2[:, t, :], st2[:, t, :])
                link(ins)
                link(v.tensor_scalar(mv2[:, :, 1], mv2[:, :, 1], EPS, None, ALU.add))
                v.wait_ge(end_act, 2)
                link(v.reciprocal(rs2[:], rs2[:]))
                for t in range(B * TILES):
                    ins = v.tensor_scalar(x_tok[:, t, :], h_tok[:, t, :], mv2[:, t, 0:1], rs2[:, t:t + 1],
                                          ALU.subtract, ALU.mult)
                link(ins)


def mamba_stage(nc, T, shared):
    x_tok, ident = shared["x_tok"], shared["ident"]
    LAYERS, DM = T["in_w"].shape[0], T["in_w"].shape[1]
    DT = T["in_w"].shape[2] // 2 // P
    NST = T["A_log"].shape[2]
    BP = B // 2
    W2 = 2 * S
    TP = W2 // P
    KC = T["cw"].shape[3]
    PAD = KC - 1

    with ExitStack() as ctx:
        def sb(name, shape, dt=F32):
            return ctx.enter_context(nc.sbuf_tensor("m_" + name, shape, dt))

        def sem(name):
            return ctx.enter_context(nc.semaphore("m_" + name))

        inw = sb("inw", [P, 2 * DT * P])
        xwB = sb("xwB", [P, DT, NST])
        xwCC = sb("xwCC", [P, DT, 2 * NST])
        dtw = sb("dtw", [P, DT, DT * P])
        outw = sb("outw", [P, DT, DM])
        convw = sb("convw", [P, DT, KC])
        convb = sb("convb", [P, DT])
        dtb = sb("dtb", [P, DT])
        dvec = sb("dvec", [P, DT])
        alog = sb("alog", [P, DT, NST])
        lng = sb("lng", [P, DM])
        lnb = sb("lnb", [P, DM])
        A = sb("A", [P, DT, NST])
        diagD = sb("diagD", [P, DT, P])
        xT = sb("xT", [P, W2])
        xm = sb("xm", [P, DT, 2, PAD + S])
        sz = sb("sz", [P, DT * W2])
        xc = sb("xc", [P, DT * W2])
        dt_ = sb("dt", [P, DT, 2, S])
        u = sb("u", [P, DT, W2])
        Bsb = sb("Bsb", [NST, W2])
        c_him = sb("c_him", [P, W2], BF16)
        c_mid = sb("c_mid", [NST, W2], BF16)
        c_lo = sb("c_lo", [NST, W2], BF16)
        sel = shared["sel"]
        Bb = sb("Bb", [P, 2, W2])
        dA = sb("dA", [P, 2, DT, 2, S])
        hs = sb("hs", [P, 2, DT * W2])
        pr = sb("pr", [P, 2, DT * W2])
        stats = sb("stats", [P, TP, 6])
        mv = sb("mv", [P, TP, 2])
        rstd = sb("rstd", [P, TP])
        Y = ctx.enter_context(nc.psum_tensor("m_Y", [P, DT * W2], F32))
        C = ctx.enter_context(nc.psum_tensor("m_C", [P, 3 * 512], F32))
        Bscr = nc.dram_tensor("m_Bscr", (NST, W2), F32, kind="Internal").ap()

        w_loaded = sem("w_loaded")
        pre_pe, pre_act, pre_dve = sem("pre_pe"), sem("pre_act"), sem("pre_dve")
        b_stored = sem("b_stored")
        b_loaded = [sem("b_loaded0"), sem("b_loaded1")]
        dbx_ready, da_ready, scan_done = sem("dbx_ready"), sem("da_ready"), sem("scan_done")
        c_ready, prod_ready, sum_done = sem("c_ready"), sem("prod_ready"), sem("sum_done")
        post_pe, post_act, post_dve = sem("post_pe"), sem("post_act"), sem("post_dve")
        waits_met = sem("waits_met")
        neg_a, stat_sem = sem("neg_a"), sem("stats_done")

        NW, N_PE, N_ACT, N_DVE = 14, 7, 11, 14
        M_DVE = 5

        def chunks(a, b):
            out = []
            while a < b:
                e = min(b, (a // 512 + 1) * 512)
                out.append((a, e))
                a = e
            return out

        def apart(eng):
            eng.sem_inc(waits_met, 1)

        CRED = 2

        with nc.Block() as block:
            @block.sync
            def _(sp):
                with sp.Fori(0, LAYERS) as L:
                    sp.wait_ge(post_dve, L * (BP * M_DVE) + 1)
                    l1 = bass.ds(L, 1)
                    for dst, src in (
                        (inw[:], T["in_w"][l1].rearrange("o k n -> (o k) n")),
                        (xwB[:], T["xw"][l1, :, 0:NST].rearrange("o (a k) n -> k (o a) n", k=P)),
                        (xwCC[:, :, 0:NST], T["xw"][l1, :, NST:2 * NST].rearrange("o (a k) n -> k (o a) n", k=P)),
                        (xwCC[:, :, NST:], T["xw"][l1, :, NST:2 * NST].rearrange("o (a k) n -> k (o a) n", k=P)),
                        (dtw[:], T["dw"][l1].rearrange("o (a k) n -> k (o a) n", k=P)),
                        (outw[:], T["ow"][l1].rearrange("o (a k) n -> k (o a) n", k=P)),
                        (convw[:], T["cw"][l1].rearrange("o k a w -> k (o a) w")),
                        (convb[:], T["cb"][l1].rearrange("o k a -> k (o a)")),
                        (dtb[:], T["db"][l1].rearrange("o k a -> k (o a)")),
                        (dvec[:], T["D"][l1].rearrange("o k a -> k (o a)")),
                        (alog[:], T["A_log"][l1].rearrange("o (a k) n -> k (o a) n", k=P)),
                        (lng[:], T["ln_g"][l1, :].to_broadcast([P, DM])),
                        (lnb[:], T["ln_b"][l1, :].to_broadcast([P, DM])),
                    ):
                        sp.dma_start(dst, src).then_inc(w_loaded, 16)
                    for bp in range(BP):
                        p = L * BP + bp
                        sp.wait_ge(pre_act, p * N_ACT + 8)
                        sp.dma_start(Bscr, Bsb[:]).then_inc(b_stored, 16)
                        sp.wait_ge(b_stored, p * 16 + 16)
                        apart(sp)
                        with sp.Fori(0, NST // 2) as i:
                            for k in range(2):
                                sp.wait_ge(dbx_ready, p * NST + i * 2 + (k + 1))
                                sp.dma_start(Bb[:, k, :], Bscr[bass.ds(i * 2 + k, 1), :].to_broadcast([P, W2])
                                             ).then_inc(b_loaded[k], 16)

            @block.gpsimd
            def _(pool):
                pool.memset(xm[:], 0.0).then_inc(dbx_ready, 1)
                pool.memset(dA[:], 0.0).then_inc(dbx_ready, 1)
                with pool.Fori(0, LAYERS) as L:
                    for bp in range(BP):
                        p = L * BP + bp
                        pool.wait_ge(pre_dve, p * N_DVE + 14)
                        apart(pool)
                        with pool.Fori(0, NST // 2) as i:
                            for k in range(2):
                                n = i * 2 + k
                                pool.wait_ge(b_loaded[k], p * (NST // 2 * 16) + i * 16 + 16)
                                pool.wait_ge(prod_ready, p * NST + i * 2 + (k + 1))
                                pool.tensor_tensor(hs[:, k, :].rearrange("p (d w) -> p d w", d=DT), u[:],
                                                   Bb[:, k:k + 1, :].to_broadcast([P, DT, W2]), ALU.mult
                                                   ).then_inc(dbx_ready, 1)

            @block.scalar
            def _(act):
                with act.Fori(0, LAYERS) as L:
                    act.wait_ge(w_loaded, L * (13 * 16) + 13 * 16)
                    act.activation(A[:], alog[:], ACT.Exp).then_inc(neg_a, 1)
                    for bp in range(BP):
                        p = L * BP + bp
                        Q = p * N_ACT
                        act.wait_ge(pre_pe, p * N_PE + 1)
                        act.copy(xT[:], C[:, 0:W2]).then_inc(pre_act, 1)
                        act.wait_ge(pre_pe, p * N_PE + 2)
                        act.wait_ge(dbx_ready, CRED)
                        for d in range(DT):
                            ins = act.copy(xm[:, d, :, PAD:], Y[:, d * W2:(d + 1) * W2].rearrange("p (b t) -> p b t", b=2))
                        ins.then_inc(pre_act, 1)
                        act.wait_ge(pre_pe, p * N_PE + 3)
                        act.activation(sz[:, 0:W2], C[:, 0:W2], ACT.Silu).then_inc(pre_act, 1)
                        act.wait_ge(pre_pe, p * N_PE + 4)
                        act.activation(sz[:, W2:2 * W2], Y[:, 0:W2], ACT.Silu).then_inc(pre_act, 1)
                        act.wait_ge(pre_dve, p * N_DVE + 10)
                        for d in range(DT):
                            ins = act.activation(xc[:, d * W2:(d + 1) * W2], pr[:, 0, d * W2:(d + 1) * W2], ACT.Silu,
                                                 bias=convb[:, d:d + 1])
                        ins.then_inc(pre_act, 1)
                        act.wait_ge(pre_pe, p * N_PE + 5)
                        act.copy(c_him[:], C[:, 0:W2]).then_inc(pre_act, 1)
                        act.wait_ge(pre_dve, p * N_DVE + 11)
                        act.copy(c_him[NST:P, :], pr[NST:P, 1, 0:W2])
                        act.copy(c_mid[:], pr[0:NST, 1, 0:W2]).then_inc(pre_act, 1)
                        act.wait_ge(pre_pe, p * N_PE + 7)
                        act.copy(Bsb[:], C[0:NST, 0:W2]).then_inc(pre_act, 1)
                        act.wait_ge(pre_pe, p * N_PE + 6)
                        for d in range(DT):
                            r = slice(d * W2, (d + 1) * W2)
                            act.activation(hs[:, 0, r], Y[:, r], ACT.Identity, bias=dtb[:, d:d + 1])
                            ins = act.activation(hs[:, 1, r], Y[:, r], ACT.Abs, bias=dtb[:, d:d + 1])
                        ins.then_inc(pre_act, 1)
                        act.wait_ge(pre_act, Q + 9)
                        act.activation(hs[:, 1, :], hs[:, 1, :], ACT.Exp, scale=-1.0).then_inc(pre_act, 1)
                        act.wait_ge(pre_act, Q + 10)
                        act.activation(hs[:, 1, :], hs[:, 1, :], ACT.Ln, bias=1.0).then_inc(pre_act, 1)
                        act.wait_ge(pre_dve, p * N_DVE + 13)
                        with act.Fori(0, NST // 2) as i:
                            for k in range(2):
                                act.wait_ge(scan_done, p * NST + i * 2 + (k + 1))
                                for d in range(DT):
                                    ins = act.activation(dA[:, k, d, :, 1:S], dt_[:, d, :, 1:S], ACT.Exp,
                                                         scale=A[:, d, bass.ds(i * 2 + k, 1)])
                                ins.then_inc(da_ready, 1)
                        act.wait_ge(post_dve, p * M_DVE + 3 + 1)
                        act.activation(rstd[:], mv[:, :, 1], ACT.Sqrt).then_inc(post_act, 1)

            @block.tensor
            def _(pe):
                def bcast_c(n):
                    for a, e in chunks(0, W2):
                        pe.matmul(C[:, a:e], sel[:, n].to_broadcast([P, P]), c_him[:, a:e], start=True, stop=False)
                        ins = pe.matmul(C[:, a:e], sel[0:NST, n].to_broadcast([NST, P]), c_lo[:, a:e],
                                        start=False, stop=True)
                    ins.then_inc(c_ready, 1)

                def sum_n(k):
                    for a, e in chunks(0, DT * W2):
                        ins = pe.matmul(Y[:, a:e], ident[:], pr[:, k, a:e], start=False, stop=False,
                                        skip_group_check=True)
                    ins.then_inc(sum_done, 1)

                with pe.Fori(0, LAYERS) as L:
                    pe.wait_ge(w_loaded, L * (13 * 16) + 13 * 16)
                    for bp in range(BP):
                        p = L * BP + bp
                        pe.wait_ge(post_dve, p * M_DVE + 1)
                        for j in range(TP):
                            ins = pe.transpose(C[:, j * P:(j + 1) * P], x_tok[:, bp * TP + j, :], ident[:])
                        ins.then_inc(pre_pe, 1)
                        pe.wait_ge(pre_act, p * N_ACT + 1)

                        def proj(dst, off, w, first=0):
                            for a, e in chunks(off, off + W2):
                                ins = pe.matmul(dst[:, a:e], w, xT[:, a - off:e - off], start=True, stop=True)
                            return ins

                        proj(Y, 0, inw[:, 0:P])
                        proj(Y, W2, inw[:, P:2 * P]).then_inc(pre_pe, 1)
                        proj(C, 0, inw[:, 2 * P:3 * P]).then_inc(pre_pe, 1)
                        pe.wait_ge(pre_act, p * N_ACT + 2)
                        proj(Y, 0, inw[:, 3 * P:4 * P]).then_inc(pre_pe, 1)

                        def proj2(dst, rows, off, w):
                            for a, e in chunks(off, off + W2):
                                for d in range(DT):
                                    ins = pe.matmul(dst[0:rows, a:e], w(d), xc[:, d * W2 + a - off:d * W2 + e - off],
                                                    start=(d == 0), stop=(d == DT - 1))
                            return ins

                        pe.wait_ge(pre_act, p * N_ACT + 5)
                        proj2(C, P, 0, lambda d: xwCC[:, d, :]).then_inc(pre_pe, 1)
                        proj2(Y, P, 0, lambda d: dtw[:, d, 0:P])
                        proj2(Y, P, W2, lambda d: dtw[:, d, P:2 * P]).then_inc(pre_pe, 1)
                        pe.wait_ge(pre_dve, p * N_DVE + 11)
                        proj2(C, NST, 0, lambda d: xwB[:, d, :]).then_inc(pre_pe, 1)
                        pe.wait_ge(pre_act, p * N_ACT + 9)
                        for a, e in chunks(0, DT * W2):
                            for a2, e2 in ((a, min(e, W2)), (max(a, W2), e)):
                                if a2 < e2:
                                    pe.matmul(Y[:, a2:e2], diagD[:, a2 // W2, :], xc[:, a2:e2], start=(a2 == a),
                                              stop=False, skip_group_check=True)
                        pe.wait_ge(pre_dve, p * N_DVE + 12)
                        bcast_c(bass.ds(0, 1))
                        with pe.Fori(0, NST // 2 - 1) as i:
                            for k in range(2):
                                pe.wait_ge(prod_ready, p * NST + i * 2 + (k + 1 + CRED))
                                bcast_c(bass.ds(i * 2 + (k + 1), 1))
                                sum_n(k)
                        pe.wait_ge(prod_ready, p * NST + (NST - 1 + CRED))
                        bcast_c(bass.ds(NST - 1, 1))
                        sum_n(0)
                        pe.wait_ge(prod_ready, p * NST + (NST + CRED))
                        sum_n(1)
                        pe.wait_ge(post_dve, p * M_DVE + 1 + 1)
                        for j in range(TP):
                            for d in range(DT):
                                ins = pe.matmul(C[:, j * P:(j + 1) * P], pr[:, 0, d * W2 + j * P:d * W2 + (j + 1) * P],
                                                outw[:, d, :], start=(d == 0), stop=(d == DT - 1))
                        ins.then_inc(post_pe, 1)

            @block.vector
            def _(v):
                v.sem_inc(post_dve, 1)
                v.memset(stats[:], 0.0).then_inc(scan_done, 1)
                v.memset(mv[:], 0.0).then_inc(scan_done, 1)
                v.memset(pr[:, 0, 8:16], 0.0).then_inc(prod_ready, 1)
                v.memset(pr[:, 0, 0:8], 0.0).then_inc(prod_ready, 1)
                v.memset(pr[:, 1, 0:8], 0.0).then_inc(sum_done, 1)
                v.memset(hs[:, 1, 0:8], 0.0).then_inc(sum_done, 1)
                v.wait_ge(sum_done, CRED)
                v.wait_ge(prod_ready, CRED)
                v.wait_ge(scan_done, CRED)
                v.wait_ge(dbx_ready, CRED)
                with v.Fori(0, LAYERS) as L:
                    v.wait_ge(w_loaded, L * (13 * 16) + 13 * 16)
                    v.wait_ge(neg_a, L * 2 + 1)
                    v.tensor_scalar(A[:], A[:], -1.0, None, ALU.mult).then_inc(neg_a, 1)
                    for bp in range(BP):
                        p = L * BP + bp
                        Q = p * N_DVE
                        for d in range(DT):
                            v.tensor_scalar(diagD[:, d, :], ident[:], dvec[:, d:d + 1], None, ALU.mult
                                            ).then_inc(pre_dve, 1)
                        v.wait_ge(pre_act, p * N_ACT + 2)
                        for q in range(KC):
                            for d in range(DT):
                                cv = pr[:, 0, d * W2:(d + 1) * W2].rearrange("p (b t) -> p b t", b=2)
                                if q == 0:
                                    ins = v.tensor_scalar(cv, xm[:, d, :, 0:S], convw[:, d, 0:1], None, ALU.mult)
                                else:
                                    v.wait_ge(pre_dve, Q + 2 + 2 * (q - 1) + d + 1)
                                    ins = v.scalar_tensor_tensor(cv, xm[:, d, :, q:q + S], convw[:, d, q:q + 1], cv,
                                                                 ALU.mult, ALU.add)
                                ins.then_inc(pre_dve, 1)
                        v.wait_ge(pre_act, p * N_ACT + 6)
                        v.tensor_tensor(pr[:, 1, 0:W2], C[:, 0:W2], c_him[:], ALU.subtract).then_inc(pre_dve, 1)
                        v.wait_ge(pre_act, p * N_ACT + 7)
                        v.tensor_tensor(c_lo[:], pr[0:NST, 1, 0:W2], c_mid[:], ALU.subtract).then_inc(pre_dve, 1)
                        v.wait_ge(pre_act, p * N_ACT + 11)
                        df = dt_[:].rearrange("p d b t -> p (d b t)")
                        v.scalar_tensor_tensor(df, hs[:, 0, :], 0.0, hs[:, 1, :], ALU.max, ALU.add
                                               ).then_inc(pre_dve, 1)
                        v.wait_ge(pre_dve, Q + 13)
                        v.tensor_tensor(u[:].rearrange("p d w -> p (d w)"), df, xc[:], ALU.mult
                                        ).then_inc(pre_dve, 1)
                        with v.Fori(0, NST // 2) as i:
                            for k in range(2):
                                g = p * NST + i * 2 + k
                                v.wait_ge(dbx_ready, p * NST + i * 2 + (k + 1 + CRED))
                                v.wait_ge(da_ready, p * NST + i * 2 + (k + 1))
                                v.tensor_tensor_scan(hs[:, k, :], dA[:, k].rearrange("p d b t -> p (d b t)"),
                                                     hs[:, k, :], 0.0, ALU.mult, ALU.add).then_inc(scan_done, 1)
                                v.wait_ge(scan_done, p * NST + i * 2 + (k + 1 + CRED))
                                v.wait_ge(c_ready, p * NST + i * 2 + (k + 1))
                                v.wait_ge(sum_done, p * NST + i * 2 + (k + 1))
                                v.tensor_tensor(pr[:, k, :].rearrange("p (d w) -> p d w", d=DT),
                                                hs[:, k, :].rearrange("p (d w) -> p d w", d=DT),
                                                C[:, 0:W2].unsqueeze(1).to_broadcast([P, DT, W2]),
                                                ALU.mult).then_inc(prod_ready, 1)
                        M = p * M_DVE
                        v.wait_ge(sum_done, p * NST + (NST + CRED))
                        v.tensor_tensor(pr[:, 0, :], Y[:], sz[:], ALU.mult).then_inc(post_dve, 1)
                        v.wait_ge(post_pe, p * 1 + 1)
                        xt = x_tok[:, bp * TP:(bp + 1) * TP, :]
                        xt2 = xt.rearrange("p j c -> p (j c)")
                        v.tensor_tensor(xt2, C[:, 0:W2], xt2, ALU.add).then_inc(post_dve, 1)
                        v.wait_ge(post_dve, M + 2 + 1)
                        for j in range(TP):
                            ins = v.bn_stats(stats[:, j, :], xt[:, j, :])
                        ins.then_inc(stat_sem, 1)
                        v.wait_ge(stat_sem, p * 4 + 1)
                        apart(v)
                        for j in range(TP):
                            ins = v.bn_aggr(mv[:, j, :], stats[:, j, :])
                        ins.then_inc(stat_sem, 1)
                        v.wait_ge(stat_sem, p * 4 + 2)
                        v.tensor_scalar(mv[:, :, 1], mv[:, :, 1], EPS, None, ALU.add).then_inc(post_dve, 1)
                        v.wait_ge(post_act, p * 1 + 1)
                        v.reciprocal(rstd[:], rstd[:]).then_inc(stat_sem, 1)
                        v.wait_ge(stat_sem, p * 4 + 3)
                        for j in range(TP):
                            ins = v.tensor_scalar(xt[:, j, :], xt[:, j, :], mv[:, j, 0:1], rstd[:, j:j + 1],
                                                  ALU.subtract, ALU.mult)
                        ins.then_inc(stat_sem, 1)
                        v.wait_ge(stat_sem, p * 4 + 4)
                        v.tensor_tensor(xt, xt, lng[:].unsqueeze(1).to_broadcast([P, TP, DM]), ALU.mult
                                        ).then_inc(post_dve, 1)
                        v.wait_ge(post_dve, M + 4 + 1)
                        v.tensor_tensor(xt, xt, lnb[:].unsqueeze(1).to_broadcast([P, TP, DM]), ALU.add
                                        ).then_inc(post_dve, 1)


def ffn_stage(nc, T, shared, out):
    h_tok, x_tok, ident = shared["h_tok"], shared["x_tok"], shared["ident"]
    DM = h_tok.shape[2]
    HEADS, HD = 8, DM // 8
    GH, SLOT = 4, 32
    GROUPS = HEADS // GH
    SCALE = float(DM) ** -0.5
    CUT = -3.0e38
    UNITS = TILES * HEADS
    VW = HD + 1

    with ExitStack() as ctx:
        def sb(name, shape, dt=F32):
            return ctx.enter_context(nc.sbuf_tensor("f_" + name, shape, dt))

        def ps(name, shape):
            return ctx.enter_context(nc.psum_tensor("f_" + name, shape, F32))

        def sem(name):
            return ctx.enter_context(nc.semaphore("f_" + name))

        wq = sb("wq", [P, GROUPS, GH, SLOT])
        wk = sb("wk", [P, GROUPS, GH, SLOT])
        wv = sb("wv", [P, DM])
        wo = sb("wo", [P, DM])
        qb = sb("qb", [P, GROUPS])
        kb = sb("kb", [P, GROUPS])
        vb = sb("vb", [P, DM])
        wob = sb("wob", [P, DM])
        taps = sb("taps", [P, 3])
        posb = sb("posb", [P, 1])
        tap1 = sb("tap1", [P, 1])
        h = sb("h", [P, TILES, DM])
        hb = sb("hb", [P, TILES, DM])
        stats = sb("stats", [P, TILES, 6])
        mv = sb("mv", [P, TILES, 2])
        rstd = sb("rstd", [P, TILES])
        xn = sb("xn", [P, TILES, DM])
        xp = sb("xp", [P, S + 2])
        x2 = sb("x2", [P, S])
        qT = sb("qT", [P, GROUPS, S])
        kT = sb("kT", [P, GROUPS, S])
        vp = sb("vp", [P, TILES, HEADS, VW])
        top1 = sb("top1", [P, 2, 8])
        top2 = sb("top2", [P, 2, 8])
        negm = sb("negm", [P, 2])
        cut1 = sb("cut1", [P, S])
        cut2 = sb("cut2", [P, 2, S])
        e_all = sb("e_all", [P, 2, S])
        e_cut = sb("e_cut", [P, 2, S])
        prob = sb("prob", [P, 2, S])
        probT = sb("probT", [P, 2, TILES, P])
        rsum = sb("rsum", [P, HEADS])
        o = sb("o", [P, DM])
        oT = sb("oT", [P, DM])
        res = sb("res", [P, TILES, DM])

        LG = ps("LG", [P, 2, 1024])
        PT = ps("PT", [P, 1024])
        O = ps("O", [P, 512])
        R = ps("R", [P, 512])
        LGf = LG[:].rearrange("p k n -> p (k n)")
        Ov = O[:, 0:HEADS * VW].rearrange("p (h w) -> p h w", w=VW)

        zeroed, w_loaded = sem("zeroed"), sem("w_loaded")
        pre_dve, pre_act, pre_pe, pre_pool = sem("pre_dve"), sem("pre_act"), sem("pre_pe"), sem("pre_pool")
        logits_ready, top_ready, neg_ready, cut1_ready = (sem(n) for n in
                                                          ("logits_ready", "top_ready", "neg_ready", "cut1_ready"))
        top2_ready, cut2_ready = sem("top2_ready"), sem("cut2_ready")
        exp_ready, expcut_ready, prob_ready = sem("exp_ready"), sem("expcut_ready"), sem("prob_ready")
        probT_ready, probT_copied, pv_done = sem("probT_ready"), sem("probT_copied"), sem("pv_done")
        o_ready, oT_ready, oT_copied, r_ready, res_ready = (sem(n) for n in
                                                            ("o_ready", "oT_ready", "oT_copied", "r_ready",
                                                             "res_ready"))
        rsum_ready, stored = sem("rsum_ready"), sem("stored")
        waits_met = sem("waits_met")
        N_DVE, N_ACT, N_PE = 12, 4, 5

        def apart(eng):
            eng.sem_inc(waits_met, 1)

        def chunks(a, b):
            out_ = []
            while a < b:
                e = min(b, (a // 512 + 1) * 512)
                out_.append((a, e))
                a = e
            return out_

        with nc.Block() as block:
            @block.sync
            def _(sp):
                sp.sem_inc(stored, 1)
                sp.wait_ge(zeroed, 5)
                wT = T["qkv_wT"]

                loads = []
                for g in range(GROUPS):
                    c0 = g * GH * HD
                    loads.append((wq[:, g, :, 0:HD], wT[:, c0:c0 + GH * HD].rearrange("c (i d) -> c i d", d=HD)))
                    loads.append((wk[:, g, :, 0:HD], wT[:, DM + c0:DM + c0 + GH * HD].rearrange("c (i d) -> c i d", d=HD)))
                loads += [(wv[:], wT[:, 2 * DM:3 * DM]), (wo[:], T["wo_wT"]), (taps[:], T["pos_w"]), (posb[:], T["pos_b"]),
                          (vb[:], T["qkv_b"][2 * DM:3 * DM].unsqueeze(0).to_broadcast([P, DM])),
                          (wob[:], T["wo_b"].unsqueeze(0).to_broadcast([P, DM]))]
                for i in range(GH):
                    loads.append((qb[SLOT * i:SLOT * i + HD, :], T["qk_b"][0, i]))
                    loads.append((kb[SLOT * i:SLOT * i + HD, :], T["qk_b"][1, i]))
                assert len(loads) == 18
                for dst, src in loads:
                    sp.dma_start(dst, src).then_inc(w_loaded, 16)
                with sp.Fori(0, B) as b:
                    for j in range(TILES):
                        sp.wait_ge(res_ready, b * TILES + (j + 1) + 1)
                        sp.dma_start(out[bass.ds(b, 1), j * P:(j + 1) * P, :].rearrange("o p c -> p (o c)"), res[:, j, :]
                                     ).then_inc(stored, 16)
                sp.wait_ge(stored, B * TILES * 16 + 1)

            @block.gpsimd
            def _(pool):
                pool.memset(wq[:], 0.0).then_inc(zeroed, 1)
                pool.memset(wk[:], 0.0).then_inc(zeroed, 1)
                pool.memset(qb[:], 0.0).then_inc(zeroed, 1)
                pool.memset(kb[:], 0.0).then_inc(zeroed, 1)
                pool.memset(vp[:], 1.0).then_inc(zeroed, 1)
                pool.memset(xp[:], 0.0).then_inc(pre_pool, 1)
                pool.wait_ge(w_loaded, 18 * 16)
                pool.tensor_scalar(tap1[:], taps[:, 1:2], 1.0, None, ALU.add).then_inc(pre_pool, 1)
                with pool.Fori(0, B) as b:
                    pool.wait_ge(pre_dve, b * N_DVE + 1)
                    pool.wait_ge(res_ready, b * TILES + 1)
                    pool.tensor_tensor(hb[:], h[:], wob[:].unsqueeze(1).to_broadcast([P, TILES, DM]), ALU.add
                                       ).then_inc(pre_pool, 1)

                    def sub(c):
                        k = c % 2
                        pool.wait_ge(expcut_ready, b * UNITS + (c + 1))
                        if c >= 2:
                            pool.wait_ge(probT_ready, b * UNITS + (c - 1))
                        pool.tensor_tensor(prob[:, k, :], e_all[:, k, :], e_cut[:, k, :], ALU.subtract
                                           ).then_inc(prob_ready, 1)

                    for c in range(UNITS):
                        k = c % 2
                        pool.wait_ge(top_ready, b * UNITS + (c + 1))
                        if c >= 2:
                            pool.wait_ge(exp_ready, b * UNITS + (c - 1))
                        apart(pool)
                        pool.tensor_scalar(negm[:, k:k + 1], top1[:, k, 0:1], -1.0, None, ALU.mult).then_inc(neg_ready, 1)
                        if c >= 1:
                            sub(c - 1)
                    sub(UNITS - 1)

            @block.scalar
            def _(act):
                act.wait_ge(w_loaded, 18 * 16)
                with act.Fori(0, B) as b:
                    act.wait_ge(pre_dve, b * N_DVE + 4)
                    act.activation(rstd[:], mv[:, :, 1], ACT.Sqrt).then_inc(pre_act, 1)
                    act.wait_ge(pre_pe, b * N_PE + 1)
                    act.wait_ge(pre_pool, 2)
                    act.copy(xp[:, 1:S + 1], LGf[:, 0:S]).then_inc(pre_act, 1)
                    act.wait_ge(pre_pe, b * N_PE + 3)
                    for g in range(GROUPS):
                        act.wait_ge(pre_pe, b * N_PE + 3 + g)
                        act.activation(kT[:, g, :], PT[:, 0:S], ACT.Identity, bias=kb[:, g:g + 1]).then_inc(pre_act, 1)

                    def probT_copy(c):
                        k = c % 2
                        act.wait_ge(probT_ready, b * UNITS + (c + 1))
                        if c >= 2:
                            act.wait_ge(pv_done, b * UNITS + (c - 1))
                        act.copy(probT[:, k].rearrange("p j q -> p (j q)"), PT[:, 0:S]).then_inc(probT_copied, 1)

                    def exp_cut(c):
                        k = c % 2
                        act.wait_ge(cut2_ready, b * UNITS + (c + 1))
                        if c >= 2:
                            act.wait_ge(prob_ready, b * UNITS + (c - 1))
                        act.activation(e_cut[:, k, :], cut2[:, k, :], ACT.Exp, bias=negm[:, k:k + 1]
                                       ).then_inc(expcut_ready, 1)

                    def o_copy(t):
                        act.wait_ge(oT_ready, b * TILES + (t + 1))
                        act.copy(oT[:], R[:, 0:DM]).then_inc(oT_copied, 1)

                    for c in range(UNITS + 4):
                        k = c % 2
                        if 1 <= c <= UNITS:
                            exp_cut(c - 1)
                        if c < UNITS:
                            act.wait_ge(neg_ready, b * UNITS + (c + 1))
                            act.wait_ge(cut1_ready, b * UNITS + (c + 1))
                            if c >= 2:
                                act.wait_ge(prob_ready, b * UNITS + (c - 1))
                            act.activation(e_all[:, k, :], LG[:, k, 0:S], ACT.Exp, bias=negm[:, k:k + 1]
                                           ).then_inc(exp_ready, 1)
                        if 2 <= c < UNITS + 2:
                            probT_copy(c - 2)
                        if c >= HEADS + 3 and (c - HEADS - 3) % HEADS == 0:
                            o_copy((c - HEADS - 3) // HEADS)

            @block.tensor
            def _(pe):
                pe.wait_ge(w_loaded, 18 * 16)
                with pe.Fori(0, B) as b:
                    pe.wait_ge(pre_dve, b * N_DVE + 6)
                    for j in range(TILES):
                        ins = pe.transpose(LGf[:, j * P:(j + 1) * P], xn[:, j, :], ident[:])
                    ins.then_inc(pre_pe, 1)
                    pe.wait_ge(pre_dve, b * N_DVE + 9)

                    def proj(dst, off, w):
                        for a, e in chunks(off, off + S):
                            ins = pe.matmul(dst[:, a:e], w, x2[:, a - off:e - off], start=True, stop=True)
                        return ins

                    for g in range(GROUPS):
                        ins = proj(LGf, g * S, wq[:, g].rearrange("p i s -> p (i s)"))
                    ins.then_inc(pre_pe, 1)
                    proj(PT, 0, wk[:, 0].rearrange("p i s -> p (i s)")).then_inc(pre_pe, 1)
                    pe.wait_ge(pre_act, b * N_ACT + 3)
                    proj(PT, 0, wk[:, 1].rearrange("p i s -> p (i s)")).then_inc(pre_pe, 1)
                    pe.wait_ge(pre_dve, b * N_DVE + 11)
                    for j in range(TILES):
                        ins = pe.matmul(LGf[:, j * P:(j + 1) * P], x2[:, j * P:(j + 1) * P], wv[:], start=True, stop=True)
                    ins.then_inc(pre_pe, 1)
                    pe.wait_ge(pre_dve, b * N_DVE + 12)
                    pe.wait_ge(pre_act, b * N_ACT + 4)

                    def logits(c):
                        t, hd, k = c // HEADS, c % HEADS, c % 2
                        g, i = hd // GH, hd % GH
                        if c >= 2:
                            pe.wait_ge(cut1_ready, b * UNITS + (c - 1))
                            pe.wait_ge(exp_ready, b * UNITS + (c - 1))
                        r = slice(SLOT * i, SLOT * i + SLOT)
                        for a, e in chunks(0, S):
                            ins = pe.matmul(LG[:, k, a:e], qT[r, g, t * P:(t + 1) * P], kT[r, g, a:e], start=True, stop=True)
                        ins.then_inc(logits_ready, 1)

                    def transposes(c):
                        k = c % 2
                        pe.wait_ge(prob_ready, b * UNITS + (c + 1))
                        if c >= 1:
                            pe.wait_ge(probT_copied, b * UNITS + c)
                        for j in range(TILES):
                            ins = pe.transpose(PT[:, j * P:(j + 1) * P], prob[:, k, j * P:(j + 1) * P], ident[:])
                        ins.then_inc(probT_ready, 1)

                    def pv(c):
                        t, hd, k = c // HEADS, c % HEADS, c % 2
                        pe.wait_ge(probT_copied, b * UNITS + (c + 1))
                        if hd == 0 and t >= 1:
                            pe.wait_ge(o_ready, b * TILES + t)
                        for j in range(TILES):
                            ins = pe.matmul(Ov[:, hd, :], probT[:, k, j, :], vp[:, j, hd, :],
                                            start=(j == 0), stop=(j == TILES - 1))
                        ins.then_inc(pv_done, 1)

                    def o_out(t, step):
                        if step == 0:
                            pe.wait_ge(o_ready, b * TILES + (t + 1))
                            if t >= 1:
                                pe.wait_ge(res_ready, b * TILES + t + 1)
                            pe.transpose(R[:, 0:DM], o[:], ident[:]).then_inc(oT_ready, 1)
                        else:
                            pe.wait_ge(oT_copied, b * TILES + (t + 1))
                            pe.matmul(R[:, DM:2 * DM], oT[:], wo[:], start=True, stop=True).then_inc(r_ready, 1)

                    logits(0)
                    for c in range(UNITS + 5):
                        if c + 1 < UNITS:
                            logits(c + 1)
                        if 2 <= c < UNITS + 2:
                            transposes(c - 2)
                        if 3 <= c < UNITS + 3:
                            pv(c - 3)
                        if c >= HEADS + 3 and (c - HEADS - 3) % HEADS == 0:
                            o_out((c - HEADS - 3) // HEADS, 0)
                        if c >= HEADS + 4 and (c - HEADS - 4) % HEADS == 0:
                            o_out((c - HEADS - 4) // HEADS, 1)

            @block.vector
            def _(v):
                v.sem_inc(res_ready, 1)
                v.wait_ge(w_loaded, 18 * 16)
                v.wait_ge(pre_pool, 2)
                with v.Fori(0, B) as b:
                    D0 = b * N_DVE
                    bt = bass.ds(b * TILES, TILES)
                    v.wait_ge(pre_pool, b + 2)
                    v.tensor_tensor(h[:], h_tok[:, bt, :], x_tok[:, bt, :], ALU.add).then_inc(pre_dve, 1)
                    v.wait_ge(pre_dve, D0 + 1)
                    for j in range(TILES):
                        ins = v.bn_stats(stats[:, j, :], h[:, j, :])
                    ins.then_inc(pre_dve, 1)
                    v.wait_ge(pre_dve, D0 + 2)
                    apart(v)
                    for j in range(TILES):
                        ins = v.bn_aggr(mv[:, j, :], stats[:, j, :])
                    ins.then_inc(pre_dve, 1)
                    v.wait_ge(pre_dve, D0 + 3)
                    v.tensor_scalar(mv[:, :, 1], mv[:, :, 1], EPS, None, ALU.add).then_inc(pre_dve, 1)
                    v.wait_ge(pre_act, b * N_ACT + 1)
                    v.reciprocal(rstd[:], rstd[:]).then_inc(pre_dve, 1)
                    v.wait_ge(pre_dve, D0 + 5)
                    for j in range(TILES):
                        ins = v.tensor_scalar(xn[:, j, :], h[:, j, :], mv[:, j, 0:1], rstd[:, j:j + 1],
                                              ALU.subtract, ALU.mult)
                    ins.then_inc(pre_dve, 1)
                    v.wait_ge(pre_act, b * N_ACT + 2)
                    v.tensor_scalar(x2[:], xp[:, 0:S], taps[:, 0:1], posb[:, 0:1], ALU.mult, ALU.add
                                    ).then_inc(pre_dve, 1)
                    v.wait_ge(pre_dve, D0 + 7)
                    v.scalar_tensor_tensor(x2[:], xp[:, 1:S + 1], tap1[:, 0:1], x2[:], ALU.mult, ALU.add
                                           ).then_inc(pre_dve, 1)
                    v.wait_ge(pre_dve, D0 + 8)
                    v.scalar_tensor_tensor(x2[:], xp[:, 2:S + 2], taps[:, 2:3], x2[:], ALU.mult, ALU.add
                                           ).then_inc(pre_dve, 1)
                    v.wait_ge(pre_pe, b * N_PE + 2)
                    for g in range(GROUPS):
                        v.tensor_scalar(qT[:, g, :], LGf[:, g * S:(g + 1) * S], qb[:, g:g + 1], SCALE,
                                        ALU.add, ALU.mult).then_inc(pre_dve, 1)
                    v.wait_ge(pre_pe, b * N_PE + 5)
                    for j in range(TILES):
                        ins = v.tensor_tensor(vp[:, j, :, 0:HD], LGf[:, j * P:(j + 1) * P].rearrange("p (h d) -> p h d", d=HD),
                                              vb[:].rearrange("p (h d) -> p h d", d=HD), ALU.add)
                    ins.then_inc(pre_dve, 1)

                    def finish_a(t):
                        v.wait_ge(pv_done, b * UNITS + (t + 1) * HEADS)
                        v.reciprocal(rsum[:], Ov[:, :, HD]).then_inc(rsum_ready, 1)
                        v.wait_ge(rsum_ready, b * TILES + (t + 1))
                        if t >= 1:
                            v.wait_ge(oT_ready, b * TILES + t)
                        v.tensor_tensor(o[:].rearrange("p (h d) -> p h d", d=HD), Ov[:, :, 0:HD],
                                        rsum[:].unsqueeze(2).to_broadcast([P, HEADS, HD]), ALU.mult
                                        ).then_inc(o_ready, 1)

                    def finish_b(t):
                        v.wait_ge(r_ready, b * TILES + (t + 1))
                        v.wait_ge(stored, b * (TILES * 16) + 1)
                        v.wait_ge(pre_pool, b + 3)
                        v.tensor_tensor(res[:, t, :], R[:, DM:2 * DM], hb[:, t, :], ALU.add).then_inc(res_ready, 1)

                    for c in range(UNITS + 6):
                        k = c % 2
                        if c < UNITS:
                            g0 = b * UNITS
                            v.wait_ge(logits_ready, g0 + (c + 1))
                            if c >= 2:
                                v.wait_ge(neg_ready, g0 + (c - 1))
                            apart(v)
                            v.max(top1[:, k, :], LG[:, k, 0:S]).then_inc(top_ready, 1)
                            v.wait_ge(top_ready, g0 + (c + 1))
                            if c >= 1:
                                v.wait_ge(cut2_ready, g0 + c)
                            apart(v)
                            v.match_replace(cut1[:], top1[:, k, :], LG[:, k, 0:S], CUT).then_inc(cut1_ready, 1)
                            v.wait_ge(cut1_ready, g0 + (c + 1))
                            apart(v)
                            v.max(top2[:, k, :], cut1[:]).then_inc(top2_ready, 1)
                            v.wait_ge(top2_ready, g0 + (c + 1))
                            if c >= 2:
                                v.wait_ge(expcut_ready, g0 + (c - 1))
                            apart(v)
                            v.match_replace(cut2[:, k, :], top2[:, k, :], cut1[:], CUT).then_inc(cut2_ready, 1)
                        if c >= HEADS + 2 and (c - HEADS - 2) % HEADS == 0:
                            finish_a((c - HEADS - 2) // HEADS)
                        if c >= HEADS + 4 and (c - HEADS - 4) % HEADS == 0:
                            finish_b((c - HEADS - 4) // HEADS)


def build(nc, T, out):
    DM = T["fpW"].shape[1]
    NST = T["A_log"].shape[2]
    with ExitStack() as ctx:
        h_tok = ctx.enter_context(nc.sbuf_tensor("h_tok", [P, B * TILES, DM], F32))
        x_tok = ctx.enter_context(nc.sbuf_tensor("x_tok", [P, B * TILES, DM], F32))
        ident = ctx.enter_context(nc.sbuf_tensor("ident", [P, P], F32))
        sel = ctx.enter_context(nc.sbuf_tensor("sel", [P, NST], BF16))
        blank = ctx.enter_context(nc.semaphore("blank"))
        with nc.Block() as block:
            @block.gpsimd
            def _(pool):
                pool.memset(ident[:], 0.0).then_inc(blank, 1)
                pool.memset(sel[:], 0.0).then_inc(blank, 1)
                pool.wait_ge(blank, 2)
                pool.affine_select(out=ident[:], in_=ident[:], compare_op=ALU.not_equal, fill=1.0, base=0,
                                   pattern=[[-1, P]], channel_multiplier=1).then_inc(blank, 1)
                for n in range(P // NST):
                    pool.wait_ge(blank, 3 + n)
                    pool.affine_select(out=sel[:], in_=sel[:], compare_op=ALU.not_equal, fill=1.0, base=-NST * n,
                                       pattern=[[-1, NST]], channel_multiplier=1).then_inc(blank, 1)
        shared = dict(h_tok=h_tok, x_tok=x_tok, ident=ident, sel=sel)
        embed_stage(nc, T, shared)
        mamba_stage(nc, T, shared)
        ffn_stage(nc, T, shared, out)


def kernel(**inputs):
    import concourse.bacc as bacc
    from concourse.bass_utils import run_bass_kernel_spmd

    a = {k: np.asarray(v) for k, v in inputs.items()}
    lay = np.ascontiguousarray

    def tok(name):
        return a["L0_tok_" + name]

    def attn(name):
        return a["L0_attn_" + name]

    def ffn(name):
        return a["L0_ffn_" + name]

    words = a["x_txt"]
    L, DI = attn("conv_w").shape[:2]
    H, HD = 8, ffn("wo_w").shape[0] // 8
    GH = 4
    arrays = {
        "xT": lay(a["x"].transpose(3, 0, 2, 1)),
        "ids": lay(words.reshape(B, -1, P).transpose(2, 0, 1).reshape(P, -1)),
        "edges": tok("edge_index"), "edgesT": lay(tok("edge_index").T),
        "table": lay(a["L0_txt_conv_w"].transpose(2, 1, 0).reshape(-1, a["L0_txt_conv_w"].shape[0])),
        "fpW": tok("fpW"), "fpb": tok("fpb"), "fng": tok("fng"), "fnb": tok("fnb"),
        "in_w": attn("in_proj_w"), "xw": attn("x_proj_w"), "dw": attn("dt_w"), "A_log": attn("A_log"),
        "ow": attn("out_w"), "ln_g": attn("ln_g"), "ln_b": attn("ln_b"),
        "cw": lay(attn("conv_w").reshape(L, DI // P, P, -1).transpose(0, 2, 1, 3)),
        "qkv_wT": lay(ffn("qkv_w").T), "wo_wT": lay(ffn("wo_w").T),
        "pos_w": lay(ffn("pos_w")[:, 0]), "pos_b": lay(ffn("pos_b")[:, None]),
        "qkv_b": ffn("qkv_b"), "wo_b": ffn("wo_b"),
        "qk_b": lay(ffn("qkv_b")[:2 * H * HD].reshape(2, H // GH, GH, HD).transpose(0, 2, 3, 1)),
    }
    for key, name in (("cb", "conv_b"), ("db", "dt_b"), ("D", "D_param")):
        arrays[key] = lay(attn(name).reshape(L, DI // P, P).transpose(0, 2, 1))
    for l in range(3):
        for name in ("W", "as", "ad", "bg", "R", "g", "b"):
            w = tok(f"{name}{l}")
            arrays[f"{name}{l}"] = w.reshape(-1) if name in ("as", "ad") else w

    nc = bacc.Bacc("TRN2", target_bir_lowering=False, num_devices=1)
    arrays = {f"in_{k}": lay(v) for k, v in arrays.items()}
    T = {k[3:]: nc.dram_tensor(k, v.shape, mybir.dt.from_np(v.dtype), kind="ExternalInput").ap()
         for k, v in arrays.items()}
    for name in ("W", "as", "ad", "bg", "R", "g", "b"):
        T[name] = [T.pop(f"{name}{l}") for l in range(3)]
    out = nc.dram_tensor("out", (B, S, T["fpW"].shape[1]), F32, kind="ExternalOutput").ap()
    build(nc, T, out)
    return run_bass_kernel_spmd(nc, [arrays], core_ids=[0]).results[0]["out"]
```
